# Optimizing a Trainium2 kernel written in Bass

```python
import numpy as np
import jax
import jax.numpy as jnp

def _softmax(x, axis=-1):
    return jax.nn.softmax(x, axis=axis)

def _gelu(x):
    return jax.nn.gelu(x, approximate=True)

def _silu(x):
    return jax.nn.silu(x)

def _sigmoid(x):
    return jax.nn.sigmoid(x)

def _layernorm(x, axis=-1, eps=1e-05):
    m = jnp.mean(x, axis=axis, keepdims=True)
    v = jnp.var(x, axis=axis, keepdims=True)
    return (x - m) / jnp.sqrt(v + eps)

def _scatter_add(tgt, idx, src, axis=0):
    return tgt.at[idx].add(src)

def _segment_sum(src, seg, n):
    return jax.ops.segment_sum(src, seg, n)
kernel_name = 'mk_dlrm_tower_d1_rec_r8_3f83d3'

def setup_inputs(seed: int=0):
    np.random.seed(seed)
    _w = jnp.asarray

    def _rec_inputs():
        import jax
        import jax.numpy as jnp
        _tk = jax.random.key(seed)
        dense_ctx = jax.random.normal(jax.random.fold_in(_tk, 190), (1024, 16), jnp.float32)
        ids = jnp.stack([jax.random.randint(jax.random.fold_in(_tk, 200 + f), (1024,), 0, v, jnp.int32) for f, v in enumerate([12500, 125000, 125000, 1250, 1250, 125000, 1000, 1250, 12500, 12500, 12500, 1000, 1250, 1250, 1250, 12500, 1000, 1000, 1250, 1000, 1000, 1000, 1000, 1250, 12500, 1250, 1250, 12500, 1250, 1250, 1000, 1000])], axis=1)
        tbl_0 = 0.05 * jax.random.normal(jax.random.fold_in(_tk, 500 + 0), (12500, 64), jnp.float32)
        tbl_1 = 0.05 * jax.random.normal(jax.random.fold_in(_tk, 500 + 1), (125000, 64), jnp.float32)
        tbl_2 = 0.05 * jax.random.normal(jax.random.fold_in(_tk, 500 + 2), (125000, 64), jnp.float32)
        tbl_3 = 0.05 * jax.random.normal(jax.random.fold_in(_tk, 500 + 3), (1250, 64), jnp.float32)
        tbl_4 = 0.05 * jax.random.normal(jax.random.fold_in(_tk, 500 + 4), (1250, 64), jnp.float32)
        tbl_5 = 0.05 * jax.random.normal(jax.random.fold_in(_tk, 500 + 5), (125000, 64), jnp.float32)
        tbl_6 = 0.05 * jax.random.normal(jax.random.fold_in(_tk, 500 + 6), (1000, 64), jnp.float32)
        tbl_7 = 0.05 * jax.random.normal(jax.random.fold_in(_tk, 500 + 7), (1250, 64), jnp.float32)
        tbl_8 = 0.05 * jax.random.normal(jax.random.fold_in(_tk, 500 + 8), (12500, 64), jnp.float32)
        tbl_9 = 0.05 * jax.random.normal(jax.random.fold_in(_tk, 500 + 9), (12500, 64), jnp.float32)
        tbl_10 = 0.05 * jax.random.normal(jax.random.fold_in(_tk, 500 + 10), (12500, 64), jnp.float32)
        tbl_11 = 0.05 * jax.random.normal(jax.random.fold_in(_tk, 500 + 11), (1000, 64), jnp.float32)
        tbl_12 = 0.05 * jax.random.normal(jax.random.fold_in(_tk, 500 + 12), (1250, 64), jnp.float32)
        tbl_13 = 0.05 * jax.random.normal(jax.random.fold_in(_tk, 500 + 13), (1250, 64), jnp.float32)
        tbl_14 = 0.05 * jax.random.normal(jax.random.fold_in(_tk, 500 + 14), (1250, 64), jnp.float32)
        tbl_15 = 0.05 * jax.random.normal(jax.random.fold_in(_tk, 500 + 15), (12500, 64), jnp.float32)
        tbl_16 = 0.05 * jax.random.normal(jax.random.fold_in(_tk, 500 + 16), (1000, 64), jnp.float32)
        tbl_17 = 0.05 * jax.random.normal(jax.random.fold_in(_tk, 500 + 17), (1000, 64), jnp.float32)
        tbl_18 = 0.05 * jax.random.normal(jax.random.fold_in(_tk, 500 + 18), (1250, 64), jnp.float32)
        tbl_19 = 0.05 * jax.random.normal(jax.random.fold_in(_tk, 500 + 19), (1000, 64), jnp.float32)
        tbl_20 = 0.05 * jax.random.normal(jax.random.fold_in(_tk, 500 + 20), (1000, 64), jnp.float32)
        tbl_21 = 0.05 * jax.random.normal(jax.random.fold_in(_tk, 500 + 21), (1000, 64), jnp.float32)
        tbl_22 = 0.05 * jax.random.normal(jax.random.fold_in(_tk, 500 + 22), (1000, 64), jnp.float32)
        tbl_23 = 0.05 * jax.random.normal(jax.random.fold_in(_tk, 500 + 23), (1250, 64), jnp.float32)
        tbl_24 = 0.05 * jax.random.normal(jax.random.fold_in(_tk, 500 + 24), (12500, 64), jnp.float32)
        tbl_25 = 0.05 * jax.random.normal(jax.random.fold_in(_tk, 500 + 25), (1250, 64), jnp.float32)
        tbl_26 = 0.05 * jax.random.normal(jax.random.fold_in(_tk, 500 + 26), (1250, 64), jnp.float32)
        tbl_27 = 0.05 * jax.random.normal(jax.random.fold_in(_tk, 500 + 27), (12500, 64), jnp.float32)
        tbl_28 = 0.05 * jax.random.normal(jax.random.fold_in(_tk, 500 + 28), (1250, 64), jnp.float32)
        tbl_29 = 0.05 * jax.random.normal(jax.random.fold_in(_tk, 500 + 29), (1250, 64), jnp.float32)
        tbl_30 = 0.05 * jax.random.normal(jax.random.fold_in(_tk, 500 + 30), (1000, 64), jnp.float32)
        tbl_31 = 0.05 * jax.random.normal(jax.random.fold_in(_tk, 500 + 31), (1000, 64), jnp.float32)
        _rk = jax.random.fold_in(_tk, 7)
        W_top1 = 0.0693375 * jax.random.normal(jax.random.fold_in(_tk, 801), (208, 512), jnp.float32)
        W_top2 = 0.0441942 * jax.random.normal(jax.random.fold_in(_tk, 802), (512, 256), jnp.float32)
        W_top3 = 0.0625 * jax.random.normal(jax.random.fold_in(_tk, 803), (256, 1), jnp.float32)
        b_top1 = jnp.zeros((512,), jnp.float32)
        b_top2 = jnp.zeros((256,), jnp.float32)
        return (dense_ctx, ids, tbl_0, tbl_1, tbl_2, tbl_3, tbl_4, tbl_5, tbl_6, tbl_7, tbl_8, tbl_9, tbl_10, tbl_11, tbl_12, tbl_13, tbl_14, tbl_15, tbl_16, tbl_17, tbl_18, tbl_19, tbl_20, tbl_21, tbl_22, tbl_23, tbl_24, tbl_25, tbl_26, tbl_27, tbl_28, tbl_29, tbl_30, tbl_31, W_top1, b_top1, W_top2, b_top2, W_top3)
    dense_ctx, ids, tbl_0, tbl_1, tbl_2, tbl_3, tbl_4, tbl_5, tbl_6, tbl_7, tbl_8, tbl_9, tbl_10, tbl_11, tbl_12, tbl_13, tbl_14, tbl_15, tbl_16, tbl_17, tbl_18, tbl_19, tbl_20, tbl_21, tbl_22, tbl_23, tbl_24, tbl_25, tbl_26, tbl_27, tbl_28, tbl_29, tbl_30, tbl_31, W_top1, b_top1, W_top2, b_top2, W_top3 = _rec_inputs()

    def _L0_rec_setup():
        import jax, jax.numpy as jnp
        import numpy as np
        F0 = 32
        D = 64
        B = 256

        def _cin_layer(h, h0, W, b):
            Hn = h.shape[1]
            Mn = h0.shape[1]
            Wr = W.reshape(W.shape[0], Hn, Mn)
            x = jnp.einsum('bhd,bmd,ohm->bod', h, h0, Wr) + b[None, :, None]
            return jax.nn.relu(x)
        key = jax.random.key(seed)
        k1, k2, k3 = jax.random.split(key, 3)
        inputs = jax.random.normal(k1, (B, F0, D), dtype=jnp.float32)
        W1 = jax.random.normal(k2, (128, F0 * F0), dtype=jnp.float32) * (1.0 / np.sqrt(F0 * F0))
        b1 = jnp.zeros((128,), dtype=jnp.float32)
        W2 = jax.random.normal(k3, (128, 64 * F0), dtype=jnp.float32) * (1.0 / np.sqrt(64 * F0))
        b2 = jnp.zeros((128,), dtype=jnp.float32)
        return {'inputs': inputs, 'W1': W1, 'b1': b1, 'W2': W2, 'b2': b2}
    _L0_rec_all = _L0_rec_setup()
    _L0_rec_in = {k: v for k, v in _L0_rec_all.items() if k in ('W1', 'b1', 'W2', 'b2')}
    del _L0_rec_all
    return {'dense_ctx': dense_ctx, 'ids': ids, 'tbl_0': tbl_0, 'tbl_1': tbl_1, 'tbl_2': tbl_2, 'tbl_3': tbl_3, 'tbl_4': tbl_4, 'tbl_5': tbl_5, 'tbl_6': tbl_6, 'tbl_7': tbl_7, 'tbl_8': tbl_8, 'tbl_9': tbl_9, 'tbl_10': tbl_10, 'tbl_11': tbl_11, 'tbl_12': tbl_12, 'tbl_13': tbl_13, 'tbl_14': tbl_14, 'tbl_15': tbl_15, 'tbl_16': tbl_16, 'tbl_17': tbl_17, 'tbl_18': tbl_18, 'tbl_19': tbl_19, 'tbl_20': tbl_20, 'tbl_21': tbl_21, 'tbl_22': tbl_22, 'tbl_23': tbl_23, 'tbl_24': tbl_24, 'tbl_25': tbl_25, 'tbl_26': tbl_26, 'tbl_27': tbl_27, 'tbl_28': tbl_28, 'tbl_29': tbl_29, 'tbl_30': tbl_30, 'tbl_31': tbl_31, 'W_top1': W_top1, 'b_top1': b_top1, 'W_top2': W_top2, 'b_top2': b_top2, 'W_top3': W_top3, 'L0_rec_W1': _L0_rec_in['W1'], 'L0_rec_b1': _L0_rec_in['b1'], 'L0_rec_W2': _L0_rec_in['W2'], 'L0_rec_b2': _L0_rec_in['b2']}

def reference(dense_ctx, ids, tbl_0, tbl_1, tbl_2, tbl_3, tbl_4, tbl_5, tbl_6, tbl_7, tbl_8, tbl_9, tbl_10, tbl_11, tbl_12, tbl_13, tbl_14, tbl_15, tbl_16, tbl_17, tbl_18, tbl_19, tbl_20, tbl_21, tbl_22, tbl_23, tbl_24, tbl_25, tbl_26, tbl_27, tbl_28, tbl_29, tbl_30, tbl_31, W_top1, b_top1, W_top2, b_top2, W_top3, L0_rec_W1, L0_rec_b1, L0_rec_W2, L0_rec_b2):
    import jax
    import jax.numpy as jnp

    def _L0_rec_ref(inputs, W1, b1, W2, b2):
        import jax, jax.numpy as jnp
        import numpy as np
        F0 = 32
        D = 64
        B = 256

        def _cin_layer(h, h0, W, b):
            Hn = h.shape[1]
            Mn = h0.shape[1]
            Wr = W.reshape(W.shape[0], Hn, Mn)
            x = jnp.einsum('bhd,bmd,ohm->bod', h, h0, Wr) + b[None, :, None]
            return jax.nn.relu(x)
        h0 = inputs
        x1 = _cin_layer(h0, h0, W1, b1)
        next_hidden = x1[:, :64]
        direct1 = x1[:, 64:]
        direct2 = _cin_layer(next_hidden, h0, W2, b2)
        result = jnp.concatenate([direct1, direct2], axis=1)
        return jnp.sum(result, axis=-1)
    e = jnp.stack([tbl_0[ids[:, 0]], tbl_1[ids[:, 1]], tbl_2[ids[:, 2]], tbl_3[ids[:, 3]], tbl_4[ids[:, 4]], tbl_5[ids[:, 5]], tbl_6[ids[:, 6]], tbl_7[ids[:, 7]], tbl_8[ids[:, 8]], tbl_9[ids[:, 9]], tbl_10[ids[:, 10]], tbl_11[ids[:, 11]], tbl_12[ids[:, 12]], tbl_13[ids[:, 13]], tbl_14[ids[:, 14]], tbl_15[ids[:, 15]], tbl_16[ids[:, 16]], tbl_17[ids[:, 17]], tbl_18[ids[:, 18]], tbl_19[ids[:, 19]], tbl_20[ids[:, 20]], tbl_21[ids[:, 21]], tbl_22[ids[:, 22]], tbl_23[ids[:, 23]], tbl_24[ids[:, 24]], tbl_25[ids[:, 25]], tbl_26[ids[:, 26]], tbl_27[ids[:, 27]], tbl_28[ids[:, 28]], tbl_29[ids[:, 29]], tbl_30[ids[:, 30]], tbl_31[ids[:, 31]]], axis=1)
    z = _L0_rec_ref(e, L0_rec_W1, L0_rec_b1, L0_rec_W2, L0_rec_b2)
    z = z.reshape(z.shape[0], -1)
    h = jnp.concatenate([z, dense_ctx], axis=1)
    h = jnp.maximum(h @ W_top1 + b_top1, 0.0)
    h = jnp.maximum(h @ W_top2 + b_top2, 0.0)
    y = h @ W_top3
    return y

_drawn_inputs = setup_inputs


def setup_inputs(seed=0):
    import zlib

    import numpy as np

    out = dict(_drawn_inputs(seed))
    spreads = {'b_top1': (0.0, 2.0),
     'b_top2': (0.0, 2.0),
     'L0_rec_b1': (0.0, 0.318),
     'L0_rec_b2': (0.0, 0.714)}
    factors = {'tbl_0': 8.0,
     'tbl_1': 8.0,
     'tbl_2': 8.0,
     'tbl_3': 8.0,
     'tbl_4': 8.0,
     'tbl_5': 8.0,
     'tbl_6': 8.0,
     'tbl_7': 8.0,
     'tbl_8': 8.0,
     'tbl_9': 8.0,
     'tbl_10': 8.0,
     'tbl_11': 8.0,
     'tbl_12': 8.0,
     'tbl_13': 8.0,
     'tbl_14': 8.0,
     'tbl_15': 8.0,
     'tbl_16': 8.0,
     'tbl_17': 8.0,
     'tbl_18': 8.0,
     'tbl_19': 8.0,
     'tbl_20': 8.0,
     'tbl_21': 8.0,
     'tbl_22': 8.0,
     'tbl_23': 8.0,
     'tbl_24': 8.0,
     'tbl_25': 8.0,
     'tbl_26': 8.0,
     'tbl_27': 8.0,
     'tbl_28': 8.0,
     'tbl_29': 8.0,
     'tbl_30': 8.0,
     'tbl_31': 8.0,
     'L0_rec_W1': 8.0,
     'L0_rec_W2': 8.0,
     'dense_ctx': 8.0}
    for name, (base, spread) in spreads.items():
        noise = np.random.default_rng([zlib.crc32(name.encode()), seed]).standard_normal(out[name].shape)
        drawn = base * np.exp(spread * noise) if base else spread * noise
        out[name] = jnp.asarray(drawn.astype(out[name].dtype))
    for name, factor in factors.items():
        out[name] = (out[name] * factor).astype(out[name].dtype)
    return out
```

```python
from contextlib import ExitStack

import concourse.bass as bass
from concourse import mybir

F32 = mybir.dt.float32
BF16 = mybir.dt.bfloat16
I32 = mybir.dt.int32
U32 = mybir.dt.uint32
ALU = mybir.AluOpType
ACT = mybir.ActivationFunctionType
AX_X = mybir.AxisListType.X

P = 128
FIELDS = 32
D = 64
NB = 1024
TILES = NB // P
DD = 4
N = DD * P
PER_TILE = D // DD
CHUNKS = TILES * PER_TILE
HID = 64
CIN = 128
DENSE = 16
TOP1, TOP2 = 512, 256
PARTS = 3
YS, XS = 4, 4
BETA = (31, 30, 16, 13)
B16 = 2
RING = 10
L2G = 4
PER = 3 * L2G + YS + 1 + L2G
MT1, MT2 = TOP1 // P, TOP2 // P
HALF = 512


def first_product(c):
    return c * PER + YS + 1


def dlrm_tower(nc, dense, ids, tables, W_top1, b_top1, W_top2, b_top2, W_top3,
               W1a, W1b, b1, W2, b2, identity, select, out):
    with ExitStack() as ctx:
        def sb(name, shape, dt=F32):
            return ctx.enter_context(nc.sbuf_tensor(name, shape, dt))

        def sem(name):
            return ctx.enter_context(nc.semaphore(name))

        idx = sb("idx", [P, TILES, FIELDS], I32)
        emb = sb("emb", [P, FIELDS, TILES * D])
        ident = sb("ident", [P, P])
        sel32 = sb("sel32", [PARTS * FIELDS, YS + 1, P])
        sel = sb("sel", [PARTS * FIELDS, YS + 1, P], BF16)
        identb = sb("identb", [P, P], BF16)
        w1t = sb("w1t", [P, YS + 1, CIN])
        w2t = sb("w2t", [P, YS * XS, CIN])
        w1s = sb("w1s", [P, YS, CIN])
        bias1 = sb("bias1", [P, 1])
        bias2 = sb("bias2", [P, 1])
        parts = sb("parts", [P, DD, PARTS, FIELDS], BF16)
        rest = sb("rest", [P, DD, FIELDS])
        stack = sb("stack", [PARTS * FIELDS, 2, N], BF16)
        bsb = sb("bsb", [P, 2, N])
        work = sb("work", [P, (RING + 2 * XS) * N])
        prod = work[:, 0:RING * N].rearrange("p (r n) -> p r n", n=N)
        xr = work[:, RING * N:].rearrange("p (c a n) -> p c a n", c=2, a=XS)
        p16 = sb("p16", [P, N])
        d1 = sb("d1", [P, N])
        d2 = sb("d2", [P, N])
        z1 = sb("z1", [P, TILES * N])
        z2 = sb("z2", [P, TILES * N])
        za = sb("za", [P, NB])
        zb = sb("zb", [P, NB])
        wt1 = sb("wt1", [P, 2, TOP1])
        wt2 = sb("wt2", [P, MT1, TOP2])
        wt3 = sb("wt3", [P, MT2])
        bt1 = sb("bt1", [P, MT1])
        bt2 = sb("bt2", [P, MT2])
        ysb = sb("ysb", [1, NB])
        flat = emb[:, :, :].rearrange("p f n -> p (f n)")
        h1 = flat[:, 0:MT1 * NB].rearrange("p (m n) -> p m n", m=MT1)
        h2 = flat[:, MT1 * NB:(MT1 + MT2) * NB].rearrange("p (m n) -> p m n", m=MT2)

        ybank = ctx.enter_context(nc.psum_tensor("ybank", [P, YS + 1, N], F32))
        misc = ctx.enter_context(nc.psum_tensor("misc", [P, N], F32))
        acc2 = ctx.enter_context(nc.psum_tensor("acc2", [P, 2, N], F32))
        misc_b = misc[:, :].bitcast(BF16)

        def ytile(j, parity):
            return ybank[:, YS if j == 0 and parity else j, :]

        s_idx = sem("s_idx")
        s_const = sem("s_const")
        s_w = sem("s_w")
        s_top = sem("s_top")
        s_gath = [sem(f"s_gath{t}") for t in range(TILES)]
        s_rows = sem("s_rows")
        s_zero = sem("s_zero")
        s_cast = sem("s_cast")
        s_w1 = sem("s_w1")
        s_hi = sem("s_hi")
        s_rest = sem("s_rest")
        s_mid = sem("s_mid")
        s_parts = sem("s_parts")
        s_tp = sem("s_tp")
        s_stack = sem("s_stack")
        s_bgen = sem("s_bgen")
        s_b = sem("s_b")
        s_y = sem("s_y")
        s_prod = sem("s_prod")
        s_used = sem("s_used")
        s_x = sem("s_x")
        s_shuf = sem("s_shuf")
        s_d1 = sem("s_d1")
        s_d2 = sem("s_d2")
        s_z1 = sem("s_z1")
        s_z2 = sem("s_z2")
        s_zf = sem("s_zf")
        s_mm = sem("s_mm")
        s_act = sem("s_act")
        s_out = sem("s_out")

        block = ctx.enter_context(nc.Block())

        @block.sync
        def _(sp):
            sp.dma_start(idx[:, :, :], ids.rearrange("(t p) f -> p t f", p=P)).then_inc(s_idx, 16)
            sp.dma_start(ident[:, :], identity).then_inc(s_const, 16)
            sp.dma_start(sel32[:, :, :], select.rearrange("p (j n) -> p j n", n=P)).then_inc(s_const, 16)
            sp.dma_start(w1t[:, :, :], W1a.rearrange("p (t o) -> p t o", o=CIN)).then_inc(s_w, 16)
            sp.dma_start(w1s[:, :, :], W1b.rearrange("p (t o) -> p t o", o=CIN)).then_inc(s_w, 16)
            sp.dma_start(w2t[:, :, :], W2.rearrange("p (t o) -> p t o", o=CIN)).then_inc(s_w, 16)
            sp.dma_start(bias1[:, :], b1).then_inc(s_w, 16)
            sp.dma_start(bias2[:, :], b2).then_inc(s_w, 16)
            sp.wait_ge(s_zero, 3)
            z_rows = HID + CIN
            sp.dma_start(wt1[HID:P, 0, :], W_top1[0:HID, :]).then_inc(s_top, 16)
            sp.dma_start(wt1[:, 1, :], W_top1[HID:z_rows, :]).then_inc(s_top, 16)
            sp.dma_start(wt1[0:DENSE, 0, :], W_top1[z_rows:z_rows + DENSE, :]).then_inc(s_top, 16)
            sp.dma_start(wt2[:, :, :], W_top2.rearrange("(k p) n -> p k n", p=P)).then_inc(s_top, 16)
            sp.dma_start(wt3[:, :], W_top3).then_inc(s_top, 16)
            sp.dma_start(bt1[:, :], b_top1).then_inc(s_top, 16)
            sp.dma_start(bt2[:, :], b_top2).then_inc(s_top, 16)
            sp.dma_start(za[0:DENSE, :], dense).then_inc(s_top, 16)
            for t in range(TILES):
                sp.wait_ge(s_gath[t], 16 * FIELDS)
                sp.sem_inc(s_rows, PER_TILE)
            sp.wait_ge(s_act, 2 * (MT1 + MT2 + 1))
            sp.dma_start(out.rearrange("b o -> o b"), ysb[0:1, :]).then_inc(s_out, 16)
            sp.wait_ge(s_out, 16)

        @block.gpsimd
        def _(pool):
            pool.wait_ge(s_idx, 16)
            for t in range(TILES):
                for f in range(FIELDS):
                    nc.gpsimd.indirect_dma_start(
                        emb[:, f, t * D:(t + 1) * D], None, tables[f],
                        bass.IndirectOffsetOnAxis(idx[:, t, f:f + 1].bitcast(U32), 0)).then_inc(s_gath[t], 16)

        def transpose_parts(pe, c):
            pe.wait_ge(s_parts, c + 1)
            for dd in range(DD):
                last = nc.tensor.transpose(misc_b[0:PARTS * FIELDS, dd * P:(dd + 1) * P],
                                           parts[:, dd, :, :].rearrange("p k f -> p (k f)"), identb[:, :])
            last.then_inc(s_tp, 1)

        def make_y(j, parity):
            nc.tensor.matmul(ytile(j, parity), sel[:, j, :], stack[:, parity, :],
                             start=True, stop=True).then_inc(s_y, 1)

        def make_b(pe, c, parity):
            pe.wait_ge(s_stack, c + 1)
            nc.tensor.matmul(misc[:, :], sel[:, YS, :], stack[:, parity, :],
                             start=True, stop=True).then_inc(s_bgen, 1)

        def layer1(pe, c, before):
            pe.wait_ge(s_b, c + 1)
            for j in range(YS):
                pe.wait_ge(s_prod, before + j + 1)
                nc.tensor.matmul(misc[:, :], w1t[:, j, :], prod[:, (12 + j) % RING, :],
                                 start=(j == 0), stop=False).then_inc(s_used, 1)
            pe.wait_ge(s_prod, before + YS + 1)
            nc.tensor.matmul(misc[:, :], w1t[:, YS, :], p16[:, :], start=False, stop=True).then_inc(s_used, 1)

        def layer2_group(pe, c, parity, j, slot, before, start, stop):
            for a in range(XS):
                pe.wait_ge(s_prod, before + a + 1)
                nc.tensor.matmul(acc2[:, parity, :], w2t[:, j * XS + a, :], prod[:, (slot + a) % RING, :],
                                 start=(start and a == 0), stop=(stop and a == XS - 1)).then_inc(s_used, 1)

        @block.tensor
        def _(pe):
            pe.wait_ge(s_const, 32)
            pe.wait_ge(s_w, 16 * 5)
            pe.wait_ge(s_w1, 2)
            pe.wait_ge(s_cast, 2)
            transpose_parts(pe, 0)
            make_b(pe, 0, 0)
            for j in range(YS):
                make_y(j, 0)
            layer1(pe, 0, 0)
            pe.wait_ge(s_x, 2)
            pe.wait_ge(s_d1, 1)
            transpose_parts(pe, 1)

            def iteration(c, parity, last1=False, last2=False, start2=True):
                at = first_product(c)
                if start2:
                    pe.wait_ge(s_d2, c - 1)
                layer2_group(pe, c, parity, 1, 0, at, True, False)
                if not last1:
                    make_b(pe, c + 1, 1 - parity)
                    make_y(0, 1 - parity)
                    pe.wait_ge(s_prod, at + L2G)
                    make_y(1, 1 - parity)
                layer2_group(pe, c, parity, 2, L2G, at + L2G, False, False)
                if not last1:
                    pe.wait_ge(s_prod, at + 2 * L2G)
                    make_y(2, 1 - parity)
                layer2_group(pe, c, parity, 3, 2 * L2G, at + 2 * L2G, False, False)
                if not last1:
                    pe.wait_ge(s_prod, at + 3 * L2G)
                    make_y(3, 1 - parity)
                    layer1(pe, c + 1, at + 3 * L2G)
                skip = 0 if last1 else YS + 1
                layer2_group(pe, c, parity, 0, 3 * L2G + YS, at + 3 * L2G + skip, False, True)
                if not last2:
                    pe.wait_ge(s_x, 2 * c + 4)
                    pe.wait_ge(s_d1, c + 2)
                    transpose_parts(pe, c + 2)

            iteration(0, 0, start2=False)
            iteration(1, 1, start2=False)
            with pe.Fori(2, CHUNKS - 3, 2) as c:
                iteration(c, 0)
                iteration(c + 1, 1)
            iteration(CHUNKS - 2, 0, last2=True)
            iteration(CHUNKS - 1, 1, last1=True, last2=True)

            pe.wait_ge(s_top, 16 * 8)
            n = 0
            for half in range(NB // HALF):
                cols = slice(half * HALF, (half + 1) * HALF)
                pe.wait_ge(s_zf, 2 * (half + 1))
                for m in range(MT1):
                    if n >= YS:
                        pe.wait_ge(s_act, n - YS + 1)
                    for k, z in enumerate((za, zb)):
                        last = nc.tensor.matmul(ybank[:, n % YS, :], wt1[:, k, m * P:(m + 1) * P], z[:, cols],
                                                start=(k == 0), stop=(k == 1))
                    last.then_inc(s_mm, 1)
                    n += 1
                for m in range(MT2):
                    pe.wait_ge(s_act, n)
                    for k in range(MT1):
                        last = nc.tensor.matmul(ybank[:, n % YS, :], wt2[:, k, m * P:(m + 1) * P],
                                                h1[:, k, cols], start=(k == 0), stop=(k == MT1 - 1))
                    last.then_inc(s_mm, 1)
                    n += 1
                pe.wait_ge(s_act, n)
                for k in range(MT2):
                    last = nc.tensor.matmul(ybank[0:1, n % YS, :], wt3[:, k:k + 1], h2[:, k, cols],
                                            start=(k == 0), stop=(k == MT2 - 1))
                last.then_inc(s_mm, 1)
                n += 1

        def chunk_rows(c):
            return emb[:, :, bass.ds(c * DD, DD)].rearrange("p f d -> p d f")

        def split_high(act, c):
            act.wait_ge(s_rows, c + 1)
            act.wait_ge(s_tp, c)
            nc.scalar.copy(parts[:, :, 0, :], chunk_rows(c)).then_inc(s_hi, 1)

        def split_middle(act, c):
            act.wait_ge(s_rest, c + 1)
            nc.scalar.copy(parts[:, :, 1, :], rest[:, :, :]).then_inc(s_mid, 1)

        def copy_stack(act, c, parity):
            act.wait_ge(s_tp, c + 1)
            nc.scalar.copy(stack[:, parity, :], misc_b[0:PARTS * FIELDS, 0:N]).then_inc(s_stack, 1)

        def copy_b(act, c, parity):
            act.wait_ge(s_bgen, c + 1)
            nc.scalar.copy(bsb[:, parity, :], misc[:, :]).then_inc(s_b, 1)

        def relu1(act, c, parity, before, first=False):
            act.wait_ge(s_used, before + YS + 1)
            for half in range(2):
                nc.scalar.activation(xr[half * HID:(half + 1) * HID, parity, 0, :], misc[0:HID, :], ACT.Relu,
                                     bias=bias1[0:HID, :]).then_inc(s_x, 1)
            if not first:
                act.wait_ge(s_z1, c)
            nc.scalar.activation(d1[HID:P, :], misc[HID:P, :], ACT.Relu, bias=bias1[HID:P, :]).then_inc(s_d1, 1)

        @block.scalar
        def _(act):
            act.wait_ge(s_const, 32)
            nc.scalar.copy(identb[:, :], ident[:, :]).then_inc(s_cast, 1)
            nc.scalar.copy(sel[:, :, :], sel32[:, :, :]).then_inc(s_cast, 1)
            act.wait_ge(s_w, 16 * 5)
            act.wait_ge(s_rows, 1)
            nc.scalar.copy(parts[:, :, 0, :], emb[:, :, 0:DD].rearrange("p f d -> p d f")).then_inc(s_hi, 1)
            split_middle(act, 0)
            copy_stack(act, 0, 0)
            copy_b(act, 0, 0)
            split_high(act, 1)
            split_middle(act, 1)
            relu1(act, 0, 0, 0, first=True)

            def iteration(c, parity, last1=False, last2=False, first=False):
                at = first_product(c)
                if not last1:
                    copy_stack(act, c + 1, 1 - parity)
                if not last2:
                    split_high(act, c + 2)
                if not last1:
                    copy_b(act, c + 1, 1 - parity)
                if not last2:
                    split_middle(act, c + 2)
                if not last1:
                    relu1(act, c + 1, 1 - parity, at + 3 * L2G)
                act.wait_ge(s_used, at + (PER - YS - 1 if last1 else PER))
                if not first:
                    act.wait_ge(s_z2, c)
                nc.scalar.activation(d2[:, :], acc2[:, parity, :], ACT.Relu, bias=bias2[:, :]).then_inc(s_d2, 1)

            iteration(0, 0, first=True)
            iteration(1, 1)
            with act.Fori(2, CHUNKS - 3, 2) as c:
                iteration(c, 0)
                iteration(c + 1, 1)
            iteration(CHUNKS - 2, 0, last2=True)
            iteration(CHUNKS - 1, 1, last1=True, last2=True)

            act.wait_ge(s_top, 16 * 8)
            n = 0
            for half in range(NB // HALF):
                cols = slice(half * HALF, (half + 1) * HALF)
                for m in range(MT1):
                    act.wait_ge(s_mm, n + 1)
                    nc.scalar.activation(h1[:, m, cols], ybank[:, n % YS, :], ACT.Relu,
                                         bias=bt1[:, m:m + 1]).then_inc(s_act, 1)
                    n += 1
                for m in range(MT2):
                    act.wait_ge(s_mm, n + 1)
                    nc.scalar.activation(h2[:, m, cols], ybank[:, n % YS, :], ACT.Relu,
                                         bias=bt2[:, m:m + 1]).then_inc(s_act, 1)
                    n += 1
                act.wait_ge(s_mm, n + 1)
                nc.scalar.copy(ysb[0:1, cols], ybank[0:1, n % YS, :]).then_inc(s_act, 1)
                n += 1

        def split_rest(dve, c):
            dve.wait_ge(s_hi, c + 1)
            nc.vector.tensor_tensor(rest[:, :, :], chunk_rows(c), parts[:, :, 0, :], ALU.subtract)\
              .then_inc(s_rest, 1)

        def split_low(dve, c):
            dve.wait_ge(s_mid, c + 1)
            nc.vector.tensor_tensor(parts[:, :, 2, :], rest[:, :, :], parts[:, :, 1, :], ALU.subtract)\
              .then_inc(s_parts, 1)

        def products1(dve, c, parity, before, first=False):
            dve.wait_ge(s_b, c + 1)
            for j in range(YS):
                dve.wait_ge(s_y, YS * c + j + 1)
                if not first:
                    dve.wait_ge(s_used, before + j + 1 - RING)
                nc.vector.tensor_tensor(prod[:, (12 + j) % RING, :], ytile(j, parity), bsb[:, parity, :],
                                        ALU.mult).then_inc(s_prod, 1)
            rows = slice(B16 * FIELDS, (B16 + 1) * FIELDS)
            if not first:
                dve.wait_ge(s_used, before + YS + 1 - PER)
            nc.vector.tensor_tensor(p16[0:FIELDS, :], ytile(0, parity)[0:FIELDS, :], bsb[rows, parity, :],
                                    ALU.mult).then_inc(s_prod, 1)

        def products2(dve, c, parity, j, slot, before, back, shuffles=False):
            for a in range(XS):
                if shuffles and a:
                    nc.vector.stream_shuffle(xr[:, parity, a, :], xr[:, parity, 0, :],
                                             [(i + a) % FIELDS for i in range(FIELDS)]).then_inc(s_shuf, 1)
                    dve.wait_ge(s_shuf, c * (XS - 1) + a)
                if back:
                    dve.wait_ge(s_used, before + a + 1 - back)
                nc.vector.tensor_tensor(prod[:, (slot + a) % RING, :], ytile(j, parity), xr[:, parity, a, :],
                                        ALU.mult).then_inc(s_prod, 1)

        def add_z(dve, c, z, d, lo, ready, done):
            dve.wait_ge(ready, c + 1)
            if not isinstance(c, int) or c > 0:
                dve.wait_ge(done, c)
            here = z[lo:P, bass.ds(c // PER_TILE * N, N)]
            nc.vector.tensor_tensor(here, here, d[lo:P, :], ALU.add).then_inc(done, 1)

        @block.vector
        def _(dve):
            nc.vector.memset(p16[:, :], 0.0).then_inc(s_zero, 1)
            nc.vector.memset(za[:, :], 0.0).then_inc(s_zero, 1)
            nc.vector.memset(wt1[:, 0, :], 0.0).then_inc(s_zero, 1)
            nc.vector.memset(z1[:, :], 0.0).then_inc(s_zero, 1)
            nc.vector.memset(z2[:, :], 0.0).then_inc(s_zero, 1)
            dve.wait_ge(s_w, 16 * 5)
            nc.vector.tensor_tensor(w1t[:, 1:YS, :], w1t[:, 1:YS, :], w1s[:, 1:YS, :], ALU.add).then_inc(s_w1, 1)
            nc.vector.tensor_tensor(w1t[:, 0, :], w1t[:, 0, :], w1s[:, 0, :], ALU.add).then_inc(s_w1, 1)

            split_rest(dve, 0)
            split_low(dve, 0)
            dve.wait_ge(s_zero, 5)
            products1(dve, 0, 0, 0, first=True)
            split_rest(dve, 1)
            split_low(dve, 1)

            def iteration(c, parity, last1=False, last2=False, first=False):
                at = first_product(c)
                dve.wait_ge(s_x, 2 * c + 2)
                dve.wait_ge(s_y, YS * c + YS)
                products2(dve, c, parity, 1, 0, at, 0 if first else RING + 1, shuffles=True)
                if not last2:
                    split_rest(dve, c + 2)
                products2(dve, c, parity, 2, L2G, at + L2G, 0 if first else RING)
                if not last2:
                    split_low(dve, c + 2)
                products2(dve, c, parity, 3, 2 * L2G, at + 2 * L2G, RING)
                add_z(dve, c, z1, d1, HID, s_d1, s_z1)
                if not first:
                    add_z(dve, c - 1, z2, d2, 0, s_d2, s_z2)
                if not last1:
                    products1(dve, c + 1, 1 - parity, at + 3 * L2G)
                skip = 0 if last1 else YS + 1
                products2(dve, c, parity, 0, 3 * L2G + YS, at + 3 * L2G + skip, RING + 1 - (YS + 1 - skip))

            iteration(0, 0, first=True)
            iteration(1, 1)
            with dve.Fori(2, CHUNKS - 3, 2) as c:
                iteration(c, 0)
                iteration(c + 1, 1)
            iteration(CHUNKS - 2, 0, last2=True)
            iteration(CHUNKS - 1, 1, last1=True, last2=True)
            add_z(dve, CHUNKS - 1, z2, d2, 0, s_d2, s_z2)

            dve.wait_ge(s_z1, CHUNKS)
            dve.wait_ge(s_z2, CHUNKS)
            for half in range(NB // HALF):
                cols = slice(half * HALF, (half + 1) * HALF)
                wide = slice(half * HALF * DD, (half + 1) * HALF * DD)
                for z, zs, lo in ((z1, za, HID), (z2, zb, 0)):
                    nc.vector.tensor_reduce(zs[lo:P, cols].rearrange("p (t b) -> p t b", b=P),
                                            z[lo:P, wide].rearrange("p (t d b) -> p t b d", d=DD, b=P),
                                            AX_X, ALU.add).then_inc(s_zf, 1)


def kernel(**inputs):
    import numpy as np
    import concourse.bacc as bacc
    from concourse.bass_utils import run_bass_kernel_spmd

    select = np.zeros((PARTS * FIELDS, YS + 1, 4, FIELDS), np.float32)
    for j in range(YS + 1):
        for q in range(4):
            turn = BETA[q] if j == YS else 4 * j + 16 * (q // 2)
            for i in range(FIELDS):
                select[(i + turn) % FIELDS::FIELDS, j, q, i] = 1.0
    def pair_rows(q, i, j, a):
        y = (i + 4 * j + 16 * (q // 2)) % FIELDS
        return (32 * (q % 2) + (i + a) % FIELDS, y)

    q, i = (v.reshape(-1) for v in np.meshgrid(np.arange(4), np.arange(FIELDS), indexing="ij"))
    w1 = np.asarray(inputs["L0_rec_W1"]).reshape(CIN, FIELDS, FIELDS)
    w2 = np.asarray(inputs["L0_rec_W2"]).reshape(CIN, HID, FIELDS)
    w1a = np.zeros((P, YS + 1, CIN), w1.dtype)
    w1b = np.zeros((P, YS, CIN), w1.dtype)
    for j in range(YS):
        y, b = (i + 4 * j + 16 * (q // 2)) % FIELDS, (i + np.array(BETA)[q]) % FIELDS
        w1a[:, j], w1b[:, j] = w1[:, y, b].T, w1[:, b, y].T
    w1b[B16 * FIELDS:(B16 + 1) * FIELDS, 0] = 0
    first = np.arange(FIELDS)
    w1a[0:FIELDS, YS] = w1[:, first, (first + 16) % FIELDS].T
    w2p = np.stack([w2[(slice(None), *pair_rows(q, i, j, a))].T for j in range(YS) for a in range(XS)], axis=1)

    arrays = {f"tbl_{f}": np.ascontiguousarray(inputs[f"tbl_{f}"]) for f in range(FIELDS)}
    for name in ("ids", "W_top1", "W_top2"):
        arrays[name] = np.ascontiguousarray(inputs[name])
    arrays["dense"] = np.ascontiguousarray(np.asarray(inputs["dense_ctx"]).T)
    for name, parts in (("b_top1", MT1), ("b_top2", MT2), ("W_top3", MT2), ("L0_rec_b1", 1), ("L0_rec_b2", 1)):
        arrays[name] = np.ascontiguousarray(np.asarray(inputs[name]).reshape(parts, P).T)
    arrays["W1a"], arrays["W1b"], arrays["W2"] = w1a.reshape(P, -1), w1b.reshape(P, -1), w2p.reshape(P, -1)
    arrays["identity"] = np.eye(P, dtype=np.float32)
    arrays["select"] = select.reshape(PARTS * FIELDS, (YS + 1) * P)

    nc = bacc.Bacc("TRN2", target_bir_lowering=False, num_devices=1)
    aps = {name: nc.dram_tensor(f"in_{name}", a.shape, mybir.dt.from_np(a.dtype), kind="ExternalInput").ap()
           for name, a in arrays.items()}
    out = nc.dram_tensor("out", (NB, 1), F32, kind="ExternalOutput").ap()
    dlrm_tower(nc, aps["dense"], aps["ids"], [aps[f"tbl_{f}"] for f in range(FIELDS)],
               aps["W_top1"], aps["b_top1"], aps["W_top2"], aps["b_top2"], aps["W_top3"],
               aps["W1a"], aps["W1b"], aps["L0_rec_b1"], aps["W2"], aps["L0_rec_b2"],
               aps["identity"], aps["select"], out)
    r = run_bass_kernel_spmd(nc, [{f"in_{name}": a for name, a in arrays.items()}], core_ids=[0])
    return r.results[0]["out"]
```

```python
from contextlib import ExitStack

import concourse.bass as bass
from concourse import mybir

F32 = mybir.dt.float32
F32R = mybir.dt.float32r
BF16 = mybir.dt.bfloat16
I32 = mybir.dt.int32
U32 = mybir.dt.uint32
ALU = mybir.AluOpType
ACT = mybir.ActivationFunctionType
AX_X = mybir.AxisListType.X

P = 128
FIELDS = 32
D = 64
NB = 1024
TILES = NB // P
DD = 4
N = DD * P
PER_TILE = D // DD
CHUNKS = TILES * PER_TILE
HID = 64
CIN = 128
DENSE = 16
TOP1, TOP2 = 512, 256
PARTS = 3
YS, XS = 4, 4
BETA = (31, 30, 16, 13)
B16 = 2
SPLIT = XS - 1
E_WHOLE = 3
WHOLE_RING = 10
RAW_RING = 10
PART_RING = 10
WHOLE = (YS - 1) + YS + E_WHOLE
L1_AT = YS - 1
PARTS_AFTER = 7
Y_FROM = (2, 3, 4)
L1_AFTER = (3, 3, 4, 4)
PAIRS = (YS - 1) * SPLIT + 1
GATHER_IN = PER_TILE - 3
EMB_TILES = 2
MT1, MT2 = TOP1 // P, TOP2 // P
HALF = 512


def whole_before(c):
    return c * WHOLE + YS


def dlrm_tower(nc, dense, ids, tables, W_top1, b_top1, W_top2, b_top2, W_top3,
               W1a, W1b, b1, W2, b2, identity, select, out):
    with ExitStack() as ctx:
        def sb(name, shape, dt=F32):
            return ctx.enter_context(nc.sbuf_tensor(name, shape, dt))

        def sem(name):
            return ctx.enter_context(nc.semaphore(name))

        idx = sb("idx", [P, TILES, FIELDS], I32)
        idxs = sb("idxs", [P, FIELDS], I32)
        land = sb("land", [P, FIELDS, D])
        emb = sb("emb", [P, FIELDS, EMB_TILES * D])
        ident = sb("ident", [P, P])
        sel = sb("sel", [PARTS * FIELDS, YS + 1, P], BF16)
        identb = sb("identb", [P, P], BF16)
        w1t = sb("w1t", [P, YS + 1, CIN])
        w2t = sb("w2t", [P, YS * XS, CIN])
        w16h = sb("w16h", [P, CIN], F32R)
        w16l = sb("w16l", [P, CIN], F32R)
        bias1 = sb("bias1", [P, 1])
        bias2 = sb("bias2", [P, 1])
        parts = sb("parts", [P, DD, PARTS, FIELDS], BF16)
        rest = sb("rest", [P, DD, FIELDS])
        stack = sb("stack", [PARTS * FIELDS, 2, N], BF16)
        bsb = sb("bsb", [P, 2, N])
        w2h = sb("w2h", [P, PAIRS, CIN], F32R)
        w2l = sb("w2l", [P, PAIRS, CIN], F32R)
        whole = sb("whole", [P, WHOLE_RING, N])
        raw = sb("raw", [P, RAW_RING, N])
        high = sb("high", [P, PART_RING, N], F32R)
        low = sb("low", [P, PART_RING, N], F32R)
        xr = sb("xr", [P, 2, XS, N])
        raw16 = sb("raw16", [FIELDS, N])
        p16 = sb("p16", [P, N], F32R)
        d1 = sb("d1", [P, N])
        d2 = sb("d2", [P, N])
        z1 = sb("z1", [P, TILES * N])
        z2 = sb("z2", [P, TILES * N])
        za = sb("za", [P, NB])
        zb = xr[:, 0, 0:NB // N, :].rearrange("p r n -> p (r n)")
        zo = raw[:, 0:NB // N, :].rearrange("p r n -> p (r n)")
        wt1 = sb("wt1", [P, 2, TOP1])
        wt2 = sb("wt2", [P, MT1, TOP2])
        wt3 = sb("wt3", [P, MT2])
        bt1 = sb("bt1", [P, MT1])
        bt2 = sb("bt2", [P, MT2])
        ysb = land[0:1, :, :].rearrange("p f d -> p (f d)")[:, 0:NB]
        h1, h2 = whole[:, 0:MT1, :], whole[:, MT1:MT1 + MT2, :]
        w1s = whole[:, WHOLE_RING - 3, :].rearrange("p (j o) -> p j o", o=CIN)
        sel32 = whole[0:PARTS * FIELDS, WHOLE_RING - 2:, :].rearrange("p r n -> p (r n)")[:, 0:(YS + 1) * P]\
            .rearrange("p (j n) -> p j n", n=P)

        ybank = ctx.enter_context(nc.psum_tensor("ybank", [P, YS + 1, N], F32))
        misc = ctx.enter_context(nc.psum_tensor("misc", [P, N], F32))
        acc2 = ctx.enter_context(nc.psum_tensor("acc2", [P, 2, N], F32))
        misc_b = misc[:, :].bitcast(BF16)

        def ytile(j, parity):
            return ybank[:, YS if j == 0 and parity else j, :]

        s_idx = sem("s_idx")
        s_const = sem("s_const")
        s_w = sem("s_w")
        s_top = sem("s_top")
        s_gath = sem("s_gath")
        s_rows = sem("s_rows")
        s_idxs = sem("s_idxs")
        s_zero = sem("s_zero")
        s_cast = sem("s_cast")
        s_w1 = sem("s_w1")
        s_w2 = sem("s_w2")
        s_hi = sem("s_hi")
        s_rest = sem("s_rest")
        s_mid = sem("s_mid")
        s_parts = sem("s_parts")
        s_tp = sem("s_tp")
        s_stack = sem("s_stack")
        s_bgen = sem("s_bgen")
        s_b = sem("s_b")
        s_y = sem("s_y")
        s_whole = sem("s_whole")
        s_raw16 = sem("s_raw16")
        s_high16 = sem("s_high16")
        s_p16 = sem("s_p16")
        s_raw = sem("s_raw")
        s_high = sem("s_high")
        s_low = sem("s_low")
        s_wused = sem("s_wused")
        s_sum1 = sem("s_sum1")
        s_pused = sem("s_pused")
        s_x = sem("s_x")
        s_shuf = sem("s_shuf")
        s_d1 = sem("s_d1")
        s_d2 = sem("s_d2")
        s_z1 = sem("s_z1")
        s_z2 = sem("s_z2")
        s_sumd = sem("s_sumd")
        s_zf = sem("s_zf")
        s_mm = sem("s_mm")
        s_act = sem("s_act")
        s_out = sem("s_out")

        block = ctx.enter_context(nc.Block())

        @block.sync
        def _(sp):
            sp.dma_start(idx[:, :, :], ids.rearrange("(t p) f -> p t f", p=P)).then_inc(s_idx, 16)
            sp.dma_start(ident[:, :], identity).then_inc(s_const, 16)
            sp.dma_start(sel32[:, :, :], select.rearrange("p (j n) -> p j n", n=P)).then_inc(s_const, 16)
            sp.dma_start(w1t[:, :, :], W1a.rearrange("p (t o) -> p t o", o=CIN)).then_inc(s_w, 16)
            sp.dma_start(w1s[:, :, :], W1b.rearrange("p (t o) -> p t o", o=CIN)).then_inc(s_w, 16)
            sp.dma_start(w2t[:, :, :], W2.rearrange("p (t o) -> p t o", o=CIN)).then_inc(s_w, 16)
            sp.dma_start(bias1[:, :], b1).then_inc(s_w, 16)
            sp.dma_start(bias2[:, :], b2).then_inc(s_w, 16)
            sp.wait_ge(s_zero, 3)
            z_rows = HID + CIN
            sp.dma_start(wt1[HID:P, 0, :], W_top1[0:HID, :]).then_inc(s_top, 16)
            sp.dma_start(wt1[:, 1, :], W_top1[HID:z_rows, :]).then_inc(s_top, 16)
            sp.dma_start(wt1[0:DENSE, 0, :], W_top1[z_rows:z_rows + DENSE, :]).then_inc(s_top, 16)
            sp.dma_start(wt2[:, :, :], W_top2.rearrange("(k p) n -> p k n", p=P)).then_inc(s_top, 16)
            sp.dma_start(wt3[:, :], W_top3).then_inc(s_top, 16)
            sp.dma_start(bt1[:, :], b_top1).then_inc(s_top, 16)
            sp.dma_start(bt2[:, :], b_top2).then_inc(s_top, 16)
            sp.dma_start(za[0:DENSE, :], dense).then_inc(s_top, 16)
            for t in range(EMB_TILES):
                sp.wait_ge(s_gath, 16 * FIELDS * (t + 1))
                sp.dma_start(emb[:, :, t * D:(t + 1) * D], land[:, :, :]).then_inc(s_rows, 16)
            with sp.Fori(EMB_TILES, TILES) as t:
                sp.wait_ge(s_gath, t * (16 * FIELDS) + 16 * FIELDS)
                sp.wait_ge(s_parts, t * PER_TILE - PER_TILE)
                sp.dma_start(emb[:, :, bass.ds(t % EMB_TILES * D, D)], land[:, :, :]).then_inc(s_rows, 16)
            sp.wait_ge(s_act, 2 * (MT1 + MT2 + 1))
            sp.dma_start(out.rearrange("b o -> o b"), ysb[0:1, :]).then_inc(s_out, 16)
            sp.wait_ge(s_out, 16)

        @block.gpsimd
        def _(pool):
            def gather(f):
                nc.gpsimd.indirect_dma_start(
                    land[:, f, :], None, tables[f],
                    bass.IndirectOffsetOnAxis(idxs[:, f:f + 1].bitcast(U32), 0)).then_inc(s_gath, 16)

            def next_rows(t):
                nc.gpsimd.tensor_copy(idxs[:, :], idx[:, t, :] if isinstance(t, int) else
                                      idx[:, bass.ds(t, 1), :].rearrange("p t f -> p (t f)")).then_inc(s_idxs, 1)

            def low_parts(c, tiles):
                for i in tiles:
                    pool.wait_ge(s_high, c * PAIRS + i + 1)
                    if not (isinstance(c, int) and c == 0 and i < PART_RING):
                        pool.wait_ge(s_pused, c * PAIRS + (i + 1 - PART_RING))
                    nc.gpsimd.tensor_tensor(low[:, i % PART_RING, :], raw[:, i % RAW_RING, :],
                                            high[:, i % PART_RING, :].bitcast(F32), ALU.subtract)\
                      .then_inc(s_low, 1)

            def iteration(c, fields):
                low_parts(c, range(PAIRS))
                for f in fields:
                    gather(f)

            pool.wait_ge(s_idx, 16)
            next_rows(0)
            pool.wait_ge(s_idxs, 1)
            for f in range(FIELDS):
                gather(f)

            def share(g):
                return range(min(g, GATHER_IN) * FIELDS // GATHER_IN, min(g + 1, GATHER_IN) * FIELDS // GATHER_IN)

            pool.wait_ge(s_rows, 16)
            next_rows(1)
            pool.wait_ge(s_idxs, 2)
            for g in range(PER_TILE):
                iteration(g, share(g))
            with pool.Fori(1, TILES - 1) as t:
                pool.wait_ge(s_rows, t * 16 + 16)
                next_rows(t + 1)
                pool.wait_ge(s_idxs, t + 2)
                for g in range(PER_TILE):
                    iteration(t * PER_TILE + g, share(g))
            with pool.Fori(CHUNKS - PER_TILE, CHUNKS) as c:
                iteration(c, ())

        def transpose_parts(pe, c):
            pe.wait_ge(s_parts, c + 1)
            for dd in range(DD):
                last = nc.tensor.transpose(misc_b[0:PARTS * FIELDS, dd * P:(dd + 1) * P],
                                           parts[:, dd, :, :].rearrange("p k f -> p (k f)"), identb[:, :])
            last.then_inc(s_tp, 1)

        def make_y(j, parity):
            nc.tensor.matmul(ytile(j, parity), sel[:, j, :], stack[:, parity, :],
                             start=True, stop=True).then_inc(s_y, 1)

        def make_b(pe, c, parity):
            pe.wait_ge(s_stack, c + 1)
            nc.tensor.matmul(misc[:, :], sel[:, YS, :], stack[:, parity, :],
                             start=True, stop=True).then_inc(s_bgen, 1)

        def use_whole(pe, before, k, psum, weights, start, stop=False):
            pe.wait_ge(s_whole, before + k + 1)
            nc.tensor.matmul(psum, weights, whole[:, (k - L1_AT) % WHOLE_RING, :], start=start, stop=stop)\
              .then_inc(s_wused, 1)

        def use_p16(pe, c):
            pe.wait_ge(s_p16, c + 1)
            nc.tensor.matmul(misc[:, :], w16h[:, :], p16[:, :], start=False, stop=False)
            nc.tensor.matmul(misc[:, :], w16l[:, :], p16[:, :], start=False, stop=True).then_inc(s_sum1, 1)

        def use_split(pe, c, k, psum, last=False):
            slot = k % PART_RING
            pe.wait_ge(s_high, c * PAIRS + k + 1)
            nc.tensor.matmul(psum, w2h[:, k, :], high[:, slot, :], start=False, stop=False)
            nc.tensor.matmul(psum, w2l[:, k, :], high[:, slot, :], start=False, stop=False)
            pe.wait_ge(s_low, c * PAIRS + k + 1)
            nc.tensor.matmul(psum, w2h[:, k, :], low[:, slot, :], start=False, stop=last)\
              .then_inc(s_pused, 1)

        @block.tensor
        def _(pe):
            pe.wait_ge(s_const, 32)
            pe.wait_ge(s_w, 16 * 5)
            pe.wait_ge(s_w1, 2)
            pe.wait_ge(s_w2, 6)
            pe.wait_ge(s_cast, 2)
            transpose_parts(pe, 0)
            make_b(pe, 0, 0)
            for j in range(YS):
                make_y(j, 0)
            pe.wait_ge(s_b, 1)
            for j in range(YS):
                use_whole(pe, -L1_AT, L1_AT + j, misc[:, :], w1t[:, j, :], start=(j == 0))
            use_p16(pe, 0)

            def use_last(c, parity):
                use_split(pe, c, PAIRS - 1, acc2[:, parity, :], last=True)

            def next_parts(c):
                pe.wait_ge(s_x, 2 * c)
                pe.wait_ge(s_d1, c)
                transpose_parts(pe, c)

            next_parts(1)

            def iteration(c, parity, last=False, last2=False, first=False):
                at = whole_before(c)
                sum2 = acc2[:, parity, :]
                if not last:
                    make_b(pe, c + 1, 1 - parity)
                    make_y(0, 1 - parity)
                if not first:
                    use_last(c - 1, 1 - parity)
                for j in range(1, YS):
                    if j == 1 and not (isinstance(c, int) and c < 2):
                        pe.wait_ge(s_d2, c - 1)
                    use_whole(pe, at, j - 1, sum2, w2t[:, j * XS, :], start=(j == 1))
                for j in range(1, YS):
                    for a in range(1, XS):
                        k = (j - 1) * SPLIT + a - 1
                        if not last:
                            if k in Y_FROM:
                                turn = Y_FROM.index(k) + 1
                                pe.wait_ge(s_raw, c * PAIRS + turn * SPLIT)
                                make_y(turn, 1 - parity)
                        use_split(pe, c, k, sum2)
                        if not last and k in L1_AFTER:
                            for i in [i for i in range(YS) if L1_AFTER[i] == k]:
                                if i == 0:
                                    pe.wait_ge(s_b, c + 2)
                                use_whole(pe, at, L1_AT + i, misc[:, :], w1t[:, i, :], start=(i == 0))
                            if k == L1_AFTER[-1]:
                                use_p16(pe, c + 1)
                        if not (last or last2) and k == PARTS_AFTER:
                            next_parts(c + 2)
                for a in range(E_WHOLE):
                    use_whole(pe, at, L1_AT + (0 if last else YS) + a, sum2, w2t[:, a, :], start=False)

            iteration(0, 0, first=True)
            iteration(1, 1)
            with pe.Fori(2, CHUNKS - 3, 2) as c:
                iteration(c, 0)
                iteration(c + 1, 1)
            iteration(CHUNKS - 2, 0, last2=True)
            iteration(CHUNKS - 1, 1, last=True)
            use_last(CHUNKS - 1, 1)

            pe.wait_ge(s_top, 16 * 8)
            n = 0
            for half in range(NB // HALF):
                cols = slice(half * HALF, (half + 1) * HALF)
                pe.wait_ge(s_zf, 2 * (half + 1))
                for m in range(MT1):
                    if n >= YS:
                        pe.wait_ge(s_act, n - YS + 1)
                    for k, z in enumerate((za, zb)):
                        last = nc.tensor.matmul(ybank[:, n % YS, :], wt1[:, k, m * P:(m + 1) * P], z[:, cols],
                                                start=(k == 0), stop=(k == 1))
                    last.then_inc(s_mm, 1)
                    n += 1
                for m in range(MT2):
                    pe.wait_ge(s_act, n)
                    for k in range(MT1):
                        last = nc.tensor.matmul(ybank[:, n % YS, :], wt2[:, k, m * P:(m + 1) * P],
                                                h1[:, k, :], start=(k == 0), stop=(k == MT1 - 1))
                    last.then_inc(s_mm, 1)
                    n += 1
                pe.wait_ge(s_act, n)
                for k in range(MT2):
                    last = nc.tensor.matmul(ybank[0:1, n % YS, :], wt3[:, k:k + 1], h2[:, k, :],
                                            start=(k == 0), stop=(k == MT2 - 1))
                last.then_inc(s_mm, 1)
                n += 1

        def chunk_rows(c):
            return emb[:, :, bass.ds(c % (EMB_TILES * PER_TILE) * DD, DD)].rearrange("p f d -> p d f")

        def split_high(act, c):
            act.wait_ge(s_rows, c // PER_TILE * 16 + 16)
            act.wait_ge(s_tp, c)
            nc.scalar.copy(parts[:, :, 0, :], chunk_rows(c)).then_inc(s_hi, 1)

        def split_middle(act, c):
            act.wait_ge(s_rest, c + 1)
            nc.scalar.copy(parts[:, :, 1, :], rest[:, :, :]).then_inc(s_mid, 1)

        def copy_stack(act, c, parity):
            act.wait_ge(s_tp, c + 1)
            nc.scalar.copy(stack[:, parity, :], misc_b[0:PARTS * FIELDS, 0:N]).then_inc(s_stack, 1)

        def copy_b(act, c, parity):
            act.wait_ge(s_bgen, c + 1)
            nc.scalar.copy(bsb[:, parity, :], misc[:, :]).then_inc(s_b, 1)

        def high_part(act, c, i):
            act.wait_ge(s_raw, c * PAIRS + i + 1)
            if not (isinstance(c, int) and c == 0 and i < PART_RING):
                act.wait_ge(s_pused, c * PAIRS + (i + 1 - PART_RING))
            nc.scalar.copy(high[:, i % PART_RING, :], raw[:, i % RAW_RING, :]).then_inc(s_high, 1)

        def high16(act, c):
            act.wait_ge(s_raw16, c + 1)
            if not (isinstance(c, int) and c == 0):
                act.wait_ge(s_sum1, c)
            nc.scalar.copy(p16[0:FIELDS, :], raw16[:, :]).then_inc(s_high16, 1)

        def relu_x(act, c, parity):
            act.wait_ge(s_sum1, c + 1)
            for half in range(2):
                nc.scalar.activation(xr[half * HID:(half + 1) * HID, parity, 0, :], misc[0:HID, :], ACT.Relu,
                                     bias=bias1[0:HID, :]).then_inc(s_x, 1)

        def relu_direct(act, c, parity):
            if parity == 0 and not (isinstance(c, int) and c == 0):
                act.wait_ge(s_z1, c // 2)
            nc.scalar.activation(d1[0:HID, :] if parity else d1[HID:P, :], misc[HID:P, :], ACT.Relu, bias=bias1[HID:P, :]).then_inc(s_d1, 1)

        def relu2(act, c, parity):
            act.wait_ge(s_pused, c * PAIRS + PAIRS)
            if not (isinstance(c, int) and c == 0):
                act.wait_ge(s_z2, c)
            nc.scalar.activation(d2[:, :], acc2[:, parity, :], ACT.Relu, bias=bias2[:, :]).then_inc(s_d2, 1)

        @block.scalar
        def _(act):
            act.wait_ge(s_const, 32)
            nc.scalar.copy(identb[:, :], ident[:, :]).then_inc(s_cast, 1)
            nc.scalar.copy(sel[:, :, :], sel32[:, :, :]).then_inc(s_cast, 1)
            act.wait_ge(s_w, 16 * 5)
            act.wait_ge(s_rows, 16)
            nc.scalar.copy(parts[:, :, 0, :], emb[:, :, 0:DD].rearrange("p f d -> p d f")).then_inc(s_hi, 1)
            split_middle(act, 0)
            copy_stack(act, 0, 0)
            copy_b(act, 0, 0)
            high16(act, 0)
            split_high(act, 1)
            split_middle(act, 1)
            relu_x(act, 0, 0)
            relu_direct(act, 0, 0)
            copy_stack(act, 1, 1)

            def iteration(c, parity, last1=False, last2=False, first=False):
                for i in range(PAIRS):
                    high_part(act, c, i)
                    if i == 1 and not last2:
                        split_high(act, c + 2)
                    if i == 2 and not first:
                        relu2(act, c - 1, 1 - parity)
                    if i == 0 and not last1:
                        copy_b(act, c + 1, 1 - parity)
                    if i == 8 and not last1:
                        high16(act, c + 1)
                    if i == 8 and not last2:
                        split_middle(act, c + 2)
                if not last1:
                    relu_x(act, c + 1, 1 - parity)
                    relu_direct(act, c + 1, 1 - parity)
                if not last2:
                    copy_stack(act, c + 2, parity)

            iteration(0, 0, first=True)
            iteration(1, 1)
            with act.Fori(2, CHUNKS - 3, 2) as c:
                iteration(c, 0)
                iteration(c + 1, 1)
            iteration(CHUNKS - 2, 0, last2=True)
            iteration(CHUNKS - 1, 1, last1=True, last2=True)
            relu2(act, CHUNKS - 1, 1)

            act.wait_ge(s_top, 16 * 8)
            n = 0
            for half in range(NB // HALF):
                cols = slice(half * HALF, (half + 1) * HALF)
                for m in range(MT1):
                    act.wait_ge(s_mm, n + 1)
                    nc.scalar.activation(h1[:, m, :], ybank[:, n % YS, :], ACT.Relu,
                                         bias=bt1[:, m:m + 1]).then_inc(s_act, 1)
                    n += 1
                for m in range(MT2):
                    act.wait_ge(s_mm, n + 1)
                    nc.scalar.activation(h2[:, m, :], ybank[:, n % YS, :], ACT.Relu,
                                         bias=bt2[:, m:m + 1]).then_inc(s_act, 1)
                    n += 1
                act.wait_ge(s_mm, n + 1)
                nc.scalar.copy(ysb[0:1, cols], ybank[0:1, n % YS, :]).then_inc(s_act, 1)
                n += 1

        def split_rest(dve, c):
            dve.wait_ge(s_hi, c + 1)
            nc.vector.tensor_tensor(rest[:, :, :], chunk_rows(c), parts[:, :, 0, :], ALU.subtract)\
              .then_inc(s_rest, 1)

        def split_low(dve, c):
            dve.wait_ge(s_mid, c + 1)
            nc.vector.tensor_tensor(parts[:, :, 2, :], rest[:, :, :], parts[:, :, 1, :], ALU.subtract)\
              .then_inc(s_parts, 1)

        def make_whole(dve, before, k, y, x, wait=True):
            if wait:
                dve.wait_ge(s_wused, before + k + 1 - WHOLE_RING)
            nc.vector.tensor_tensor(whole[:, (k - L1_AT) % WHOLE_RING, :], y, x, ALU.mult).then_inc(s_whole, 1)

        def products1(dve, c, parity, before, k, first=False):
            dve.wait_ge(s_b, c + 1)
            for j in range(YS):
                dve.wait_ge(s_y, YS * c + j + 1)
                if j == 0:
                    rows = slice(B16 * FIELDS, (B16 + 1) * FIELDS)
                    nc.vector.tensor_tensor(raw16[:, :], ytile(0, parity)[0:FIELDS, :], bsb[rows, parity, :],
                                            ALU.mult).then_inc(s_raw16, 1)
                if j == 2:
                    dve.wait_ge(s_high16, c + 1)
                    nc.vector.tensor_tensor(p16[FIELDS:2 * FIELDS, :], raw16[:, :], p16[0:FIELDS, :].bitcast(F32),
                                            ALU.subtract).then_inc(s_p16, 1)
                make_whole(dve, before, k + j, ytile(j, parity), bsb[:, parity, :],
                           wait=not isinstance(c, int) or c > 1)

        def make_split(dve, c, k, y, x):
            if not (isinstance(c, int) and c == 0 and k < RAW_RING):
                dve.wait_ge(s_low, c * PAIRS + (k + 1 - RAW_RING))
            nc.vector.tensor_tensor(raw[:, k % RAW_RING, :], y, x, ALU.mult).then_inc(s_raw, 1)

        def add_z(dve, c, z, d, ready, done, before):
            dve.wait_ge(ready, c + 1)
            if not isinstance(c, int) or before > 0:
                dve.wait_ge(done, before)
            here = z[:, bass.ds(c // PER_TILE * N, N)]
            nc.vector.tensor_tensor(here, here, d[:, :], ALU.add).then_inc(done, 1)

        @block.vector
        def _(dve):
            nc.vector.memset(p16[:, :].bitcast(F32), 0.0).then_inc(s_zero, 1)
            nc.vector.memset(za[:, :], 0.0).then_inc(s_zero, 1)
            nc.vector.memset(wt1[:, 0, :], 0.0).then_inc(s_zero, 1)
            nc.vector.memset(z1[:, :], 0.0).then_inc(s_zero, 1)
            nc.vector.memset(z2[:, :], 0.0).then_inc(s_zero, 1)
            dve.wait_ge(s_w, 16 * 5)
            nc.vector.tensor_tensor(w1t[:, 1:YS, :], w1t[:, 1:YS, :], w1s[:, 1:YS, :], ALU.add).then_inc(s_w1, 1)
            nc.vector.tensor_tensor(w1t[:, 0, :], w1t[:, 0, :], w1s[:, 0, :], ALU.add).then_inc(s_w1, 1)

            triples = w2t[:, XS:, :].rearrange("p (j a) o -> p j (a o)", a=XS)[:, :, CIN:]
            in_order = [(w[:, 0:PAIRS - 1, :].rearrange("p (j a) o -> p j (a o)", a=SPLIT), w[:, PAIRS - 1, :])
                        for w in (w2h, w2l)]
            sources = (triples, w2t[:, XS - 1, :], w1t[:, YS, :])
            highs, lows = in_order[0] + (w16h[:, :],), in_order[1] + (w16l[:, :],)
            for high_w, w in zip(highs, sources):
                nc.vector.tensor_copy(high_w, w).then_inc(s_w2, 1)
            dve.wait_ge(s_w2, 3)
            for low_w, high_w, w in zip(lows, highs, sources):
                nc.vector.tensor_tensor(low_w, w, high_w.bitcast(F32), ALU.subtract).then_inc(s_w2, 1)

            split_rest(dve, 0)
            split_low(dve, 0)
            dve.wait_ge(s_zero, 5)
            products1(dve, 0, 0, -L1_AT, L1_AT, first=True)
            split_rest(dve, 1)
            split_low(dve, 1)

            def iteration(c, parity, last1=False, last2=False, first=False):
                at = whole_before(c)
                dve.wait_ge(s_x, 2 * c + 2)
                dve.wait_ge(s_y, YS * c + YS)
                def shuffle(a):
                    nc.vector.stream_shuffle(xr[:, parity, a, :], xr[:, parity, 0, :],
                                             [(i + a) % FIELDS for i in range(FIELDS)]).then_inc(s_shuf, 1)

                for j in range(1, YS):
                    if j == YS - 1:
                        shuffle(1)
                    make_whole(dve, at, j - 1, ytile(j, parity), xr[:, parity, 0, :], wait=not first)
                for j in range(1, YS):
                    for a in range(1, XS):
                        if j == 1:
                            if a + 1 < XS:
                                shuffle(a + 1)
                            dve.wait_ge(s_shuf, c * SPLIT + a)
                        make_split(dve, c, (j - 1) * SPLIT + a - 1, ytile(j, parity), xr[:, parity, a, :])
                    if j == 2 and not last2:
                        split_rest(dve, c + 2)
                if not last1:
                    products1(dve, c + 1, 1 - parity, at, L1_AT)
                make_split(dve, c, PAIRS - 1, ytile(0, parity), xr[:, parity, XS - 1, :])
                if parity:
                    add_z(dve, c, z1, d1, s_d1, s_z1, c // 2)
                if not first:
                    add_z(dve, c - 1, z2, d2, s_d2, s_z2, c - 1)
                if not last2:
                    split_low(dve, c + 2)
                skip = 0 if last1 else YS
                for a in range(E_WHOLE):
                    make_whole(dve, at, L1_AT + skip + a, ytile(0, parity), xr[:, parity, a, :])

            iteration(0, 0, first=True)
            iteration(1, 1)
            with dve.Fori(2, CHUNKS - 3, 2) as c:
                iteration(c, 0)
                iteration(c + 1, 1)
            iteration(CHUNKS - 2, 0, last2=True)
            iteration(CHUNKS - 1, 1, last1=True, last2=True)

            def sum_d(z, rows, out, to, half):
                wide = slice(half * HALF * DD, (half + 1) * HALF * DD)
                return nc.vector.tensor_reduce(
                    out[to, half * HALF:(half + 1) * HALF].rearrange("p (t b) -> p t b", b=P),
                    z[rows, wide].rearrange("p (t d b) -> p t b d", d=DD, b=P), AX_X, ALU.add)

            direct, other = slice(HID, P), slice(0, HID)
            dve.wait_ge(s_low, CHUNKS * PAIRS)
            for half in range(NB // HALF):
                cols = slice(half * HALF, (half + 1) * HALF)
                if half:
                    add_z(dve, CHUNKS - 1, z2, d2, s_d2, s_z2, CHUNKS - 1)
                dve.wait_ge(s_z1, CHUNKS // 2)
                sum_d(z1, direct, za, direct, half).then_inc(s_sumd, 1)
                sum_d(z1, other, zo, direct, half).then_inc(s_sumd, 1)
                dve.wait_ge(s_sumd, 2 * half + 2)
                nc.vector.tensor_tensor(za[direct, cols], za[direct, cols], zo[direct, cols], ALU.add)\
                  .then_inc(s_zf, 1)
                dve.wait_ge(s_z2, CHUNKS if half else CHUNKS - 1)
                sum_d(z2, slice(0, P), zb, slice(0, P), half).then_inc(s_zf, 1)


def kernel(**inputs):
    import numpy as np
    import concourse.bacc as bacc
    from concourse.bass_utils import run_bass_kernel_spmd

    select = np.zeros((PARTS * FIELDS, YS + 1, 4, FIELDS), np.float32)
    for j in range(YS + 1):
        for q in range(4):
            turn = BETA[q] if j == YS else 4 * j + 16 * (q // 2)
            for i in range(FIELDS):
                select[(i + turn) % FIELDS::FIELDS, j, q, i] = 1.0
    def pair_rows(q, i, j, a):
        y = (i + 4 * j + 16 * (q // 2)) % FIELDS
        return (32 * (q % 2) + (i + a) % FIELDS, y)

    q, i = (v.reshape(-1) for v in np.meshgrid(np.arange(4), np.arange(FIELDS), indexing="ij"))
    w1 = np.asarray(inputs["L0_rec_W1"]).reshape(CIN, FIELDS, FIELDS)
    w2 = np.asarray(inputs["L0_rec_W2"]).reshape(CIN, HID, FIELDS)
    w1a = np.zeros((P, YS + 1, CIN), w1.dtype)
    w1b = np.zeros((P, YS, CIN), w1.dtype)
    for j in range(YS):
        y, b = (i + 4 * j + 16 * (q // 2)) % FIELDS, (i + np.array(BETA)[q]) % FIELDS
        w1a[:, j], w1b[:, j] = w1[:, y, b].T, w1[:, b, y].T
    w1b[B16 * FIELDS:(B16 + 1) * FIELDS, 0] = 0
    first = np.arange(FIELDS)
    for half in range(2):
        w1a[half * FIELDS:(half + 1) * FIELDS, YS] = w1[:, first, (first + 16) % FIELDS].T
    w2p = np.stack([w2[(slice(None), *pair_rows(q, i, j, a))].T for j in range(YS) for a in range(XS)], axis=1)

    arrays = {f"tbl_{f}": np.ascontiguousarray(inputs[f"tbl_{f}"]) for f in range(FIELDS)}
    for name in ("ids", "W_top1", "W_top2"):
        arrays[name] = np.ascontiguousarray(inputs[name])
    arrays["dense"] = np.ascontiguousarray(np.asarray(inputs["dense_ctx"]).T)
    for name, parts in (("b_top1", MT1), ("b_top2", MT2), ("W_top3", MT2), ("L0_rec_b1", 1), ("L0_rec_b2", 1)):
        arrays[name] = np.ascontiguousarray(np.asarray(inputs[name]).reshape(parts, P).T)
    arrays["W1a"], arrays["W1b"], arrays["W2"] = w1a.reshape(P, -1), w1b.reshape(P, -1), w2p.reshape(P, -1)
    arrays["identity"] = np.eye(P, dtype=np.float32)
    arrays["select"] = select.reshape(PARTS * FIELDS, (YS + 1) * P)

    nc = bacc.Bacc("TRN2", target_bir_lowering=False, num_devices=1)
    aps = {name: nc.dram_tensor(f"in_{name}", a.shape, mybir.dt.from_np(a.dtype), kind="ExternalInput").ap()
           for name, a in arrays.items()}
    out = nc.dram_tensor("out", (NB, 1), F32, kind="ExternalOutput").ap()
    dlrm_tower(nc, aps["dense"], aps["ids"], [aps[f"tbl_{f}"] for f in range(FIELDS)],
               aps["W_top1"], aps["b_top1"], aps["W_top2"], aps["b_top2"], aps["W_top3"],
               aps["W1a"], aps["W1b"], aps["L0_rec_b1"], aps["W2"], aps["L0_rec_b2"],
               aps["identity"], aps["select"], out)
    r = run_bass_kernel_spmd(nc, [{f"in_{name}": a for name, a in arrays.items()}], core_ids=[0])
    return r.results[0]["out"]
```

```python
from contextlib import ExitStack

import concourse.bass as bass
from concourse import mybir

F32 = mybir.dt.float32
F32R = mybir.dt.float32r
BF16 = mybir.dt.bfloat16
I32 = mybir.dt.int32
U32 = mybir.dt.uint32
ALU = mybir.AluOpType
ACT = mybir.ActivationFunctionType
AX_X = mybir.AxisListType.X

P = 128
FIELDS = 32
D = 64
NB = 1024
TILES = NB // P
DD = 4
N = DD * P
PER_TILE = D // DD
CHUNKS = TILES * PER_TILE
HID = 64
CIN = 128
DENSE = 16
TOP1, TOP2 = 512, 256
PARTS = 3
YS, XS = 4, 4
BETA = (31, 30, 16, 13)
B16 = 2
SPLITS = ((1, 0), (1, 1), (1, 2), (1, 3), (2, 1), (2, 2), (2, 3), (3, 1), (3, 2), (3, 3), (0, 3))
PAIRS = len(SPLITS)
LAST_OF = (None, 3, 6, 9)
E_WHOLE = 3
WHOLE = 2 + YS + E_WHOLE
WHOLE_RING = WHOLE
RAW_RING = PAIRS
PART_RING = PAIRS
L1_AT = 2
PARTS_AFTER = 9
Y_FROM = (None, 1, 2, 4)
L1_AFTER = (1, 2, 5, 5)
E_AFTER = (6, 7, 8)
GATHER_IN = PER_TILE - 3
EMB_TILES = 2
MT1, MT2 = TOP1 // P, TOP2 // P
HALF = 512


def whole_summed1(c):
    return YS if isinstance(c, int) and c == 0 else whole_before(c - 1) + (L1_AT + YS)


def mlp_steps():
    ends, n = {}, 0
    for half, layer in ((0, 1), (0, 2), (1, 1), (0, 3), (1, 2), (1, 3)):
        for m in range({1: MT1, 2: MT2, 3: 1}[layer]):
            yield n, half, layer, m, max(n + 1 - YS, ends.get((half, layer - 1), 0))
            n += 1
        ends[half, layer] = n


def whole_before(c):
    return c * WHOLE + YS


def dlrm_tower(nc, dense, ids, tables, W_top1, b_top1, W_top2, b_top2, W_top3,
               W1a, W1b, b1, W2, b2, identity, select, out):
    with ExitStack() as ctx:
        def sb(name, shape, dt=F32):
            return ctx.enter_context(nc.sbuf_tensor(name, shape, dt))

        def sem(name):
            return ctx.enter_context(nc.semaphore(name))

        idx = sb("idx", [P, TILES, FIELDS], I32)
        idxs = sb("idxs", [P, FIELDS], I32)
        land = sb("land", [P, FIELDS, D])
        emb = sb("emb", [P, FIELDS, EMB_TILES * D])
        ident = sb("ident", [P, P])
        sel = sb("sel", [PARTS * FIELDS, YS + 1, P], BF16)
        identb = sb("identb", [P, P], BF16)
        w1t = sb("w1t", [P, YS + 1, CIN])
        w2t = sb("w2t", [P, YS * XS, CIN])
        w16 = sb("w16", [P, CIN], F32R)
        bias1 = sb("bias1", [P, 1])
        bias2 = sb("bias2", [P, 1])
        parts = sb("parts", [P, DD, PARTS, FIELDS], BF16)
        rest = sb("rest", [P, DD, FIELDS])
        stack_raw = sb("stack_raw", [P, 2, N], BF16)
        stack = stack_raw[0:PARTS * FIELDS, :, :]
        bsb = sb("bsb", [P, 2, N])
        w2h = sb("w2h", [P, PAIRS, CIN], F32R)
        w2l = sb("w2l", [P, PAIRS, CIN], F32R)
        whole = sb("whole", [P, WHOLE_RING, N])
        raw = sb("raw", [P, RAW_RING, N])
        high = sb("high", [P, PART_RING, N], F32R)
        low = sb("low", [P, PART_RING, N], F32R)
        xr = sb("xr", [P, 2, XS, N])
        at_again, at_low, at_high = slice(32, 64), slice(64, 96), slice(96, P)
        raw16 = stack_raw[at_high, :, :].rearrange("p s n -> p (s n)").bitcast(F32)
        p16 = sb("p16", [P, N], F32R)
        d1 = sb("d1", [P, N])
        d2 = sb("d2", [P, N])
        z1 = sb("z1", [P, TILES * N])
        z2 = sb("z2", [P, TILES * N])
        za = sb("za", [P, NB])
        zb = xr[:, 0, 0:NB // N, :].rearrange("p r n -> p (r n)")
        zo = xr[:, 0, NB // N:, :].rearrange("p r n -> p (r n)")
        wt1 = sb("wt1", [P, 2, TOP1])
        wt2 = sb("wt2", [P, MT1, TOP2])
        wt3 = sb("wt3", [P, MT2])
        bt1 = sb("bt1", [P, MT1])
        bt2 = sb("bt2", [P, MT2])
        ysb = land[0:1, :, :].rearrange("p f d -> p (f d)")[:, 0:NB]
        h1, h2 = whole[:, 0:MT1, :], whole[:, MT1:MT1 + MT2, :]
        w1s = whole[:, WHOLE_RING - 3, :].rearrange("p (j o) -> p j o", o=CIN)
        sel32 = whole[0:PARTS * FIELDS, WHOLE_RING - 2:, :].rearrange("p r n -> p (r n)")[:, 0:(YS + 1) * P]\
            .rearrange("p (j n) -> p j n", n=P)

        ybank = ctx.enter_context(nc.psum_tensor("ybank", [P, YS + 1, N], F32))
        misc = ctx.enter_context(nc.psum_tensor("misc", [P, N], F32))
        acc2 = ctx.enter_context(nc.psum_tensor("acc2", [P, 2, N], F32))
        misc_b = misc[:, :].bitcast(BF16)

        def ytile(j, parity):
            return ybank[:, YS if j == 0 and parity else j, :]

        s_idx = sem("s_idx")
        s_const = sem("s_const")
        s_w = sem("s_w")
        s_top = sem("s_top")
        s_gath = sem("s_gath")
        s_rows = sem("s_rows")
        s_idxs = sem("s_idxs")
        s_zero = sem("s_zero")
        s_cast = sem("s_cast")
        s_w1 = sem("s_w1")
        s_w2 = sem("s_w2")
        s_hi = sem("s_hi")
        s_rest = sem("s_rest")
        s_mid = sem("s_mid")
        s_parts = sem("s_parts")
        s_tp = sem("s_tp")
        s_stack = sem("s_stack")
        s_bgen = sem("s_bgen")
        s_b = sem("s_b")
        s_y = sem("s_y")
        s_whole = sem("s_whole")
        s_raw16 = sem("s_raw16")
        s_high16 = sem("s_high16")
        s_p16used = sem("s_p16used")
        s_p16 = sem("s_p16")
        s_raw = sem("s_raw")
        s_high = sem("s_high")
        s_low = sem("s_low")
        s_wused = sem("s_wused")
        s_pused = sem("s_pused")
        s_x = sem("s_x")
        s_shuf = sem("s_shuf")
        s_d1 = sem("s_d1")
        s_d2 = sem("s_d2")
        s_z1 = sem("s_z1")
        s_z2 = sem("s_z2")
        s_sumd = sem("s_sumd")
        s_zf = sem("s_zf")
        s_mm = sem("s_mm")
        s_act = sem("s_act")
        s_out = sem("s_out")

        block = ctx.enter_context(nc.Block())

        @block.sync
        def _(sp):
            sp.dma_start(idx[:, :, :], ids.rearrange("(t p) f -> p t f", p=P)).then_inc(s_idx, 16)
            sp.dma_start(ident[:, :], identity).then_inc(s_const, 16)
            sp.dma_start(sel32[:, :, :], select.rearrange("p (j n) -> p j n", n=P)).then_inc(s_const, 16)
            sp.dma_start(w1t[:, :, :], W1a.rearrange("p (t o) -> p t o", o=CIN)).then_inc(s_w, 16)
            sp.dma_start(w1s[:, :, :], W1b.rearrange("p (t o) -> p t o", o=CIN)).then_inc(s_w, 16)
            sp.dma_start(w2t[:, :, :], W2.rearrange("p (t o) -> p t o", o=CIN)).then_inc(s_w, 16)
            sp.dma_start(bias1[:, :], b1).then_inc(s_w, 16)
            sp.dma_start(bias2[:, :], b2).then_inc(s_w, 16)
            sp.wait_ge(s_zero, 3)
            z_rows = HID + CIN
            sp.dma_start(wt1[HID:P, 0, :], W_top1[0:HID, :]).then_inc(s_top, 16)
            sp.dma_start(wt1[:, 1, :], W_top1[HID:z_rows, :]).then_inc(s_top, 16)
            sp.dma_start(wt1[0:DENSE, 0, :], W_top1[z_rows:z_rows + DENSE, :]).then_inc(s_top, 16)
            sp.dma_start(wt2[:, :, :], W_top2.rearrange("(k p) n -> p k n", p=P)).then_inc(s_top, 16)
            sp.dma_start(wt3[:, :], W_top3).then_inc(s_top, 16)
            sp.dma_start(bt1[:, :], b_top1).then_inc(s_top, 16)
            sp.dma_start(bt2[:, :], b_top2).then_inc(s_top, 16)
            sp.dma_start(za[0:DENSE, :], dense).then_inc(s_top, 16)
            sp.wait_ge(s_gath, 16 * FIELDS * 2)
            sp.dma_start(emb[:, :, D:2 * D], land[:, :, :]).then_inc(s_rows, 16)
            with sp.Fori(EMB_TILES, TILES) as t:
                sp.wait_ge(s_gath, t * (16 * FIELDS) + 16 * FIELDS)
                sp.wait_ge(s_parts, t * PER_TILE - PER_TILE)
                sp.dma_start(emb[:, :, bass.ds(t % EMB_TILES * D, D)], land[:, :, :]).then_inc(s_rows, 16)
            sp.wait_ge(s_act, 2 * (MT1 + MT2 + 1))
            sp.dma_start(out.rearrange("b o -> o b"), ysb[0:1, :]).then_inc(s_out, 16)
            sp.wait_ge(s_out, 16)

        @block.gpsimd
        def _(pool):
            def gather(f, to=land):
                nc.gpsimd.indirect_dma_start(
                    to[:, f, 0:D], None, tables[f],
                    bass.IndirectOffsetOnAxis(idxs[:, f:f + 1].bitcast(U32), 0)).then_inc(s_gath, 16)

            def next_rows(t, done=s_idxs, by=1):
                nc.gpsimd.tensor_copy(idxs[:, :], idx[:, t, :] if isinstance(t, int) else
                                      idx[:, bass.ds(t, 1), :].rearrange("p t f -> p (t f)")).then_inc(done, by)

            def low_parts(c, tiles):
                for i in tiles:
                    pool.wait_ge(s_high, c * PAIRS + i + 1)
                    if not (isinstance(c, int) and c == 0 and i < PART_RING):
                        pool.wait_ge(s_pused, c * PAIRS + (i + 1 - PART_RING))
                    nc.gpsimd.tensor_tensor(low[:, i % PART_RING, :], raw[:, i % RAW_RING, :],
                                            high[:, i % PART_RING, :].bitcast(F32), ALU.subtract)\
                      .then_inc(s_low, 1)

            def iteration(c, fields):
                low_parts(c, range(PAIRS))
                for f in fields:
                    gather(f)

            pool.wait_ge(s_idx, 16)
            next_rows(0)
            pool.wait_ge(s_idxs, 1)
            for f in range(FIELDS):
                gather(f, to=emb)

            def share(g):
                return range(min(g, GATHER_IN) * FIELDS // GATHER_IN, min(g + 1, GATHER_IN) * FIELDS // GATHER_IN)

            pool.wait_ge(s_gath, 16 * FIELDS)
            next_rows(1, done=s_rows, by=16)
            pool.wait_ge(s_rows, 16)
            for g in range(PER_TILE):
                iteration(g, share(g))
            with pool.Fori(1, TILES - 1) as t:
                pool.wait_ge(s_rows, t * 16 + 16)
                next_rows(t + 1)
                pool.wait_ge(s_idxs, t + 1)
                for g in range(PER_TILE):
                    iteration(t * PER_TILE + g, share(g))
            with pool.Fori(CHUNKS - PER_TILE, CHUNKS) as c:
                iteration(c, ())

        def transpose_parts(pe, c):
            pe.wait_ge(s_parts, c + 1)
            for dd in range(DD):
                last = nc.tensor.transpose(misc_b[0:PARTS * FIELDS, dd * P:(dd + 1) * P],
                                           parts[:, dd, :, :].rearrange("p k f -> p (k f)"), identb[:, :])
            last.then_inc(s_tp, 1)

        def make_y(j, parity):
            nc.tensor.matmul(ytile(j, parity), sel[:, j, :], stack[:, parity, :],
                             start=True, stop=True).then_inc(s_y, 1)

        def make_b(pe, c, parity):
            pe.wait_ge(s_stack, c + 1)
            nc.tensor.matmul(misc[:, :], sel[:, YS, :], stack[:, parity, :],
                             start=True, stop=True).then_inc(s_bgen, 1)

        def use_whole(pe, before, k, psum, weights, start, stop=False):
            pe.wait_ge(s_whole, before + k + 1)
            nc.tensor.matmul(psum, weights, whole[:, (k - L1_AT) % WHOLE_RING, :], start=start, stop=stop)\
              .then_inc(s_wused, 1)

        def use_l1(pe, before, c, j):
            if j == 2:
                pe.wait_ge(s_p16, c + 1)
                nc.tensor.matmul(misc[:, :], w16[:, :], p16[:, :], start=False, stop=False).then_inc(s_p16used, 1)
            use_whole(pe, before, L1_AT + j, misc[:, :], w1t[:, j, :], start=(j == 0), stop=(j == YS - 1))

        def use_split(pe, c, k, psum, last=False):
            slot = k % PART_RING
            pe.wait_ge(s_high, c * PAIRS + k + 1)
            nc.tensor.matmul(psum, w2h[:, k, :], high[:, slot, :], start=False, stop=False)
            nc.tensor.matmul(psum, w2l[:, k, :], high[:, slot, :], start=False, stop=False)
            pe.wait_ge(s_low, c * PAIRS + k + 1)
            nc.tensor.matmul(psum, w2h[:, k, :], low[:, slot, :], start=False, stop=last)\
              .then_inc(s_pused, 1)

        @block.tensor
        def _(pe):
            pe.wait_ge(s_const, 32)
            pe.wait_ge(s_w, 16 * 5)
            pe.wait_ge(s_w1, 2)
            pe.wait_ge(s_w2, 10)
            pe.wait_ge(s_cast, 2)
            transpose_parts(pe, 0)
            make_b(pe, 0, 0)
            for j in range(YS):
                make_y(j, 0)
            pe.wait_ge(s_b, 1)
            for j in range(YS):
                use_l1(pe, -L1_AT, 0, j)

            def use_last(c, parity):
                use_split(pe, c, PAIRS - 1, acc2[:, parity, :], last=True)

            def next_parts(c):
                pe.wait_ge(s_x, 2 * c)
                pe.wait_ge(s_d1, c)
                transpose_parts(pe, c)

            next_parts(1)

            def iteration(c, parity, last=False, last2=False, first=False):
                at = whole_before(c)
                sum2 = acc2[:, parity, :]
                if not last:
                    make_b(pe, c + 1, 1 - parity)
                    make_y(0, 1 - parity)
                if not first:
                    use_last(c - 1, 1 - parity)
                if not (isinstance(c, int) and c < 2):
                    pe.wait_ge(s_d2, c - 1)
                for j in range(2, YS):
                    use_whole(pe, at, j - 2, sum2, w2t[:, j * XS, :], start=(j == 2))
                for k in range(PAIRS - 1):
                    if not last and k in Y_FROM:
                        j = Y_FROM.index(k)
                        pe.wait_ge(s_raw, c * PAIRS + (LAST_OF[j] + 1))
                        make_y(j, 1 - parity)
                    use_split(pe, c, k, sum2)
                    if last and k in E_AFTER:
                        use_whole(pe, at, L1_AT + E_AFTER.index(k), sum2, w2t[:, E_AFTER.index(k), :], start=False)
                    if not last and k in L1_AFTER:
                        for i in [i for i in range(YS) if L1_AFTER[i] == k]:
                            if i == 0:
                                pe.wait_ge(s_b, c + 2)
                            use_l1(pe, at, c + 1, i)
                    if not (last or last2) and k == PARTS_AFTER:
                        next_parts(c + 2)
                if not last:
                    for a in range(E_WHOLE):
                        use_whole(pe, at, L1_AT + YS + a, sum2, w2t[:, a, :], start=False)

            iteration(0, 0, first=True)
            iteration(1, 1)
            with pe.Fori(2, CHUNKS - 3, 2) as c:
                iteration(c, 0)
                iteration(c + 1, 1)
            iteration(CHUNKS - 2, 0, last2=True)
            iteration(CHUNKS - 1, 1, last=True)
            use_last(CHUNKS - 1, 1)

            pe.wait_ge(s_top, 16 * 8)
            for n, half, layer, m, needed in mlp_steps():
                if layer == 1 and m == 0:
                    pe.wait_ge(s_zf, 2 * (half + 1))
                if needed > 0:
                    pe.wait_ge(s_act, needed)
                if layer == 1:
                    cols = slice(half * HALF, (half + 1) * HALF)
                    terms = [(wt1[:, k, m * P:(m + 1) * P], z[:, cols]) for k, z in enumerate((za, zb))]
                elif layer == 2:
                    terms = [(wt2[:, k, m * P:(m + 1) * P], h1[:, k, :]) for k in range(MT1)]
                else:
                    terms = [(wt3[:, k:k + 1], h2[:, k, :]) for k in range(MT2)]
                rows = 1 if layer == 3 else P
                for k, (weights, values) in enumerate(terms):
                    done = nc.tensor.matmul(ybank[0:rows, n % YS, :], weights, values,
                                            start=(k == 0), stop=(k == len(terms) - 1))
                done.then_inc(s_mm, 1)

        def chunk_rows(c):
            return emb[:, :, bass.ds(c % (EMB_TILES * PER_TILE) * DD, DD)].rearrange("p f d -> p d f")

        def split_high(act, c):
            act.wait_ge(s_rows, c // PER_TILE * 16 + 16)
            act.wait_ge(s_tp, c)
            nc.scalar.copy(parts[:, :, 0, :], chunk_rows(c)).then_inc(s_hi, 1)

        def split_middle(act, c):
            act.wait_ge(s_rest, c + 1)
            nc.scalar.copy(parts[:, :, 1, :], rest[:, :, :]).then_inc(s_mid, 1)

        def copy_stack(act, c, parity):
            act.wait_ge(s_tp, c + 1)
            nc.scalar.copy(stack[:, parity, :], misc_b[0:PARTS * FIELDS, 0:N]).then_inc(s_stack, 1)

        def copy_b(act, c, parity):
            act.wait_ge(s_bgen, c + 1)
            nc.scalar.copy(bsb[:, parity, :], misc[:, :]).then_inc(s_b, 1)

        def high_part(act, c, i):
            act.wait_ge(s_raw, c * PAIRS + i + 1)
            if not (isinstance(c, int) and c == 0 and i < PART_RING):
                act.wait_ge(s_pused, c * PAIRS + (i + 1 - PART_RING))
            nc.scalar.copy(high[:, i % PART_RING, :], raw[:, i % RAW_RING, :]).then_inc(s_high, 1)

        def high16(act, c):
            act.wait_ge(s_raw16, c + 1)
            if not (isinstance(c, int) and c == 0):
                act.wait_ge(s_p16used, c)
            for to in (at_again, at_high):
                nc.scalar.copy(p16[to, :], raw16).then_inc(s_high16, 1)

        def relu_x(act, c, parity):
            act.wait_ge(s_wused, whole_summed1(c))
            for half in range(2):
                nc.scalar.activation(xr[half * HID:(half + 1) * HID, parity, 0, :], misc[0:HID, :], ACT.Relu,
                                     bias=bias1[0:HID, :]).then_inc(s_x, 1)

        def relu_direct(act, c, parity):
            if parity == 0 and not (isinstance(c, int) and c == 0):
                act.wait_ge(s_z1, c // 2)
            to = slice(0, HID) if parity else slice(HID, P)
            nc.scalar.activation(d1[to, :], misc[HID:P, :], ACT.Relu, bias=bias1[HID:P, :]).then_inc(s_d1, 1)

        def relu2(act, c, parity):
            act.wait_ge(s_pused, c * PAIRS + PAIRS)
            if not (isinstance(c, int) and c == 0):
                act.wait_ge(s_z2, c)
            nc.scalar.activation(d2[:, :], acc2[:, parity, :], ACT.Relu, bias=bias2[:, :]).then_inc(s_d2, 1)

        @block.scalar
        def _(act):
            act.wait_ge(s_const, 32)
            nc.scalar.copy(identb[:, :], ident[:, :]).then_inc(s_cast, 1)
            nc.scalar.copy(sel[:, :, :], sel32[:, :, :]).then_inc(s_cast, 1)
            act.wait_ge(s_w, 16 * 5)
            act.wait_ge(s_rows, 16)
            nc.scalar.copy(parts[:, :, 0, :], emb[:, :, 0:DD].rearrange("p f d -> p d f")).then_inc(s_hi, 1)
            split_middle(act, 0)
            copy_stack(act, 0, 0)
            copy_b(act, 0, 0)
            high16(act, 0)
            split_high(act, 1)
            split_middle(act, 1)
            relu_x(act, 0, 0)
            relu_direct(act, 0, 0)
            copy_stack(act, 1, 1)

            def iteration(c, parity, last1=False, last2=False, first=False):
                for i in range(PAIRS):
                    high_part(act, c, i)
                    if i == 1 and not last2:
                        split_high(act, c + 2)
                    if i == 2 and not first:
                        relu2(act, c - 1, 1 - parity)
                    if i == 0 and not last1:
                        copy_b(act, c + 1, 1 - parity)
                    if i == 6 and not last1:
                        high16(act, c + 1)
                    if i == 8 and not last2:
                        split_middle(act, c + 2)
                if not last1:
                    relu_x(act, c + 1, 1 - parity)
                    relu_direct(act, c + 1, 1 - parity)
                if not last2:
                    copy_stack(act, c + 2, parity)

            iteration(0, 0, first=True)
            iteration(1, 1)
            with act.Fori(2, CHUNKS - 3, 2) as c:
                iteration(c, 0)
                iteration(c + 1, 1)
            iteration(CHUNKS - 2, 0, last2=True)
            iteration(CHUNKS - 1, 1, last1=True, last2=True)
            relu2(act, CHUNKS - 1, 1)

            act.wait_ge(s_top, 16 * 8)
            for n, half, layer, m, _needed in mlp_steps():
                act.wait_ge(s_mm, n + 1)
                if layer == 3:
                    nc.scalar.copy(ysb[0:1, half * HALF:(half + 1) * HALF], ybank[0:1, n % YS, :]).then_inc(s_act, 1)
                else:
                    to, bias = (h1, bt1) if layer == 1 else (h2, bt2)
                    nc.scalar.activation(to[:, m, :], ybank[:, n % YS, :], ACT.Relu,
                                         bias=bias[:, m:m + 1]).then_inc(s_act, 1)

        def split_rest(dve, c):
            dve.wait_ge(s_hi, c + 1)
            nc.vector.tensor_tensor(rest[:, :, :], chunk_rows(c), parts[:, :, 0, :], ALU.subtract)\
              .then_inc(s_rest, 1)

        def split_low(dve, c):
            dve.wait_ge(s_mid, c + 1)
            nc.vector.tensor_tensor(parts[:, :, 2, :], rest[:, :, :], parts[:, :, 1, :], ALU.subtract)\
              .then_inc(s_parts, 1)

        def make_whole(dve, before, k, y, x, wait=True):
            if wait:
                dve.wait_ge(s_wused, before + k + 1 - WHOLE_RING)
            nc.vector.tensor_tensor(whole[:, (k - L1_AT) % WHOLE_RING, :], y, x, ALU.mult).then_inc(s_whole, 1)

        def product1(dve, c, parity, before, j):
            if j == 0:
                dve.wait_ge(s_b, c + 1)
            dve.wait_ge(s_y, YS * c + j + 1)
            if j == 0:
                rows = slice(B16 * FIELDS, (B16 + 1) * FIELDS)
                nc.vector.tensor_tensor(raw16, ytile(0, parity)[0:FIELDS, :], bsb[rows, parity, :],
                                        ALU.mult).then_inc(s_raw16, 1)
            if j == 2:
                dve.wait_ge(s_high16, 2 * c + 2)
                nc.vector.tensor_tensor(p16[at_low, :], raw16, p16[at_high, :].bitcast(F32),
                                        ALU.subtract).then_inc(s_p16, 1)
            make_whole(dve, before, L1_AT + j, ytile(j, parity), bsb[:, parity, :],
                       wait=not isinstance(c, int) or c > 1)

        def make_split(dve, c, k, y, x):
            if not (isinstance(c, int) and c == 0 and k < RAW_RING):
                dve.wait_ge(s_low, c * PAIRS + (k + 1 - RAW_RING))
            nc.vector.tensor_tensor(raw[:, k % RAW_RING, :], y, x, ALU.mult).then_inc(s_raw, 1)

        def add_z(dve, c, z, d, ready, done, before):
            dve.wait_ge(ready, c + 1)
            if not isinstance(c, int) or before > 0:
                dve.wait_ge(done, before)
            here = z[:, bass.ds(c // PER_TILE * N, N)]
            nc.vector.tensor_tensor(here, here, d[:, :], ALU.add).then_inc(done, 1)

        @block.vector
        def _(dve):
            nc.vector.memset(p16[0:FIELDS, :].bitcast(F32), 0.0).then_inc(s_zero, 1)
            nc.vector.memset(za[:, :], 0.0).then_inc(s_zero, 1)
            nc.vector.memset(wt1[:, 0, :], 0.0).then_inc(s_zero, 1)
            nc.vector.memset(z1[:, :], 0.0).then_inc(s_zero, 1)
            nc.vector.memset(z2[:, :], 0.0).then_inc(s_zero, 1)
            dve.wait_ge(s_w, 16 * 5)
            nc.vector.tensor_tensor(w1t[:, 1:YS, :], w1t[:, 1:YS, :], w1s[:, 1:YS, :], ALU.add).then_inc(s_w1, 1)
            nc.vector.tensor_tensor(w1t[:, 0, :], w1t[:, 0, :], w1s[:, 0, :], ALU.add).then_inc(s_w1, 1)

            runs = [(0, XS, XS), (LAST_OF[1] + 1, 2 * XS + 1, XS - 1), (LAST_OF[2] + 1, 3 * XS + 1, XS - 1),
                    (PAIRS - 1, XS - 1, 1)]
            for to, t, size in runs:
                nc.vector.tensor_copy(w2h[:, to:to + size, :], w2t[:, t:t + size, :]).then_inc(s_w2, 1)
            nc.vector.tensor_copy(w16[:, :], w1t[:, YS, :]).then_inc(s_w2, 1)
            dve.wait_ge(s_w2, len(runs) + 1)
            for to, t, size in runs:
                nc.vector.tensor_tensor(w2l[:, to:to + size, :], w2t[:, t:t + size, :],
                                        w2h[:, to:to + size, :].bitcast(F32), ALU.subtract).then_inc(s_w2, 1)
            nc.vector.tensor_tensor(w16[at_again, :], w1t[at_again, YS, :], w16[at_again, :].bitcast(F32),
                                    ALU.subtract).then_inc(s_w2, 1)

            split_rest(dve, 0)
            split_low(dve, 0)
            dve.wait_ge(s_zero, 5)
            for j in range(YS):
                product1(dve, 0, 0, -L1_AT, j)
            split_rest(dve, 1)
            split_low(dve, 1)

            def iteration(c, parity, last1=False, last2=False, first=False):
                at = whole_before(c)
                dve.wait_ge(s_x, 2 * c + 2)
                dve.wait_ge(s_y, YS * c + YS)

                def shuffle(a):
                    nc.vector.stream_shuffle(xr[:, parity, a, :], xr[:, parity, 0, :],
                                             [(i + a) % FIELDS for i in range(FIELDS)]).then_inc(s_shuf, 1)

                for k, (j, a) in enumerate(SPLITS[:-1]):
                    if j == 1 and a:
                        dve.wait_ge(s_shuf, c * (XS - 1) + a)
                    make_split(dve, c, k, ytile(j, parity), xr[:, parity, a, :])
                    if k == 0:
                        shuffle(1)
                    if k < 2:
                        make_whole(dve, at, k, ytile(k + 2, parity), xr[:, parity, 0, :], wait=not first)
                        shuffle(k + 2)
                    if not last1 and k in LAST_OF:
                        product1(dve, c + 1, 1 - parity, at, LAST_OF.index(k) - 1)
                    if k == LAST_OF[2] and not last2:
                        split_rest(dve, c + 2)
                if not last1:
                    product1(dve, c + 1, 1 - parity, at, YS - 1)
                make_split(dve, c, PAIRS - 1, ytile(0, parity), xr[:, parity, XS - 1, :])
                if parity and not last1:
                    add_z(dve, c, z1, d1, s_d1, s_z1, c // 2)
                if not (first or last1):
                    add_z(dve, c - 1, z2, d2, s_d2, s_z2, c - 1)
                if not last2:
                    split_low(dve, c + 2)
                skip = 0 if last1 else YS
                for a in range(E_WHOLE):
                    make_whole(dve, at, L1_AT + skip + a, ytile(0, parity), xr[:, parity, a, :])

            iteration(0, 0, first=True)
            iteration(1, 1)
            with dve.Fori(2, CHUNKS - 3, 2) as c:
                iteration(c, 0)
                iteration(c + 1, 1)
            iteration(CHUNKS - 2, 0, last2=True)
            iteration(CHUNKS - 1, 1, last1=True, last2=True)

            def sum_d(z, rows, out, to, half):
                wide = slice(half * HALF * DD, (half + 1) * HALF * DD)
                return nc.vector.tensor_reduce(
                    out[to, half * HALF:(half + 1) * HALF].rearrange("p (t b) -> p t b", b=P),
                    z[rows, wide].rearrange("p (t d b) -> p t b d", d=DD, b=P), AX_X, ALU.add)

            direct, other = slice(HID, P), slice(0, HID)
            for half in range(NB // HALF):
                cols = slice(half * HALF, (half + 1) * HALF)
                if half:
                    add_z(dve, CHUNKS - 1, z1, d1, s_d1, s_z1, CHUNKS // 2 - 1)
                    for c in (CHUNKS - 2, CHUNKS - 1):
                        add_z(dve, c, z2, d2, s_d2, s_z2, c)
                dve.wait_ge(s_z1, CHUNKS // 2 - 1 + half)
                sum_d(z1, direct, za, direct, half).then_inc(s_sumd, 1)
                sum_d(z1, other, zo, direct, half).then_inc(s_sumd, 1)
                dve.wait_ge(s_sumd, 2 * half + 2)
                nc.vector.tensor_tensor(za[direct, cols], za[direct, cols], zo[direct, cols], ALU.add)\
                  .then_inc(s_zf, 1)
                dve.wait_ge(s_z2, CHUNKS if half else CHUNKS - 2)
                sum_d(z2, slice(0, P), zb, slice(0, P), half).then_inc(s_zf, 1)


def kernel(**inputs):
    import numpy as np
    import concourse.bacc as bacc
    from concourse.bass_utils import run_bass_kernel_spmd

    select = np.zeros((PARTS * FIELDS, YS + 1, 4, FIELDS), np.float32)
    for j in range(YS + 1):
        for q in range(4):
            turn = BETA[q] if j == YS else 4 * j + 16 * (q // 2)
            for i in range(FIELDS):
                select[(i + turn) % FIELDS::FIELDS, j, q, i] = 1.0
    def pair_rows(q, i, j, a):
        y = (i + 4 * j + 16 * (q // 2)) % FIELDS
        return (32 * (q % 2) + (i + a) % FIELDS, y)

    q, i = (v.reshape(-1) for v in np.meshgrid(np.arange(4), np.arange(FIELDS), indexing="ij"))
    w1 = np.asarray(inputs["L0_rec_W1"]).reshape(CIN, FIELDS, FIELDS)
    w2 = np.asarray(inputs["L0_rec_W2"]).reshape(CIN, HID, FIELDS)
    w1a = np.zeros((P, YS + 1, CIN), w1.dtype)
    w1b = np.zeros((P, YS, CIN), w1.dtype)
    for j in range(YS):
        y, b = (i + 4 * j + 16 * (q // 2)) % FIELDS, (i + np.array(BETA)[q]) % FIELDS
        w1a[:, j], w1b[:, j] = w1[:, y, b].T, w1[:, b, y].T
    w1b[B16 * FIELDS:(B16 + 1) * FIELDS, 0] = 0
    first = np.arange(FIELDS)
    for part in (1, 2, 3):
        w1a[part * FIELDS:(part + 1) * FIELDS, YS] = w1[:, first, (first + 16) % FIELDS].T
    w2p = np.stack([w2[(slice(None), *pair_rows(q, i, j, a))].T for j in range(YS) for a in range(XS)], axis=1)

    arrays = {f"tbl_{f}": np.ascontiguousarray(inputs[f"tbl_{f}"]) for f in range(FIELDS)}
    for name in ("ids", "W_top1", "W_top2"):
        arrays[name] = np.ascontiguousarray(inputs[name])
    arrays["dense"] = np.ascontiguousarray(np.asarray(inputs["dense_ctx"]).T)
    for name, parts in (("b_top1", MT1), ("b_top2", MT2), ("W_top3", MT2), ("L0_rec_b1", 1), ("L0_rec_b2", 1)):
        arrays[name] = np.ascontiguousarray(np.asarray(inputs[name]).reshape(parts, P).T)
    arrays["W1a"], arrays["W1b"], arrays["W2"] = w1a.reshape(P, -1), w1b.reshape(P, -1), w2p.reshape(P, -1)
    arrays["identity"] = np.eye(P, dtype=np.float32)
    arrays["select"] = select.reshape(PARTS * FIELDS, (YS + 1) * P)

    nc = bacc.Bacc("TRN2", target_bir_lowering=False, num_devices=1)
    aps = {name: nc.dram_tensor(f"in_{name}", a.shape, mybir.dt.from_np(a.dtype), kind="ExternalInput").ap()
           for name, a in arrays.items()}
    out = nc.dram_tensor("out", (NB, 1), F32, kind="ExternalOutput").ap()
    dlrm_tower(nc, aps["dense"], aps["ids"], [aps[f"tbl_{f}"] for f in range(FIELDS)],
               aps["W_top1"], aps["b_top1"], aps["W_top2"], aps["b_top2"], aps["W_top3"],
               aps["W1a"], aps["W1b"], aps["L0_rec_b1"], aps["W2"], aps["L0_rec_b2"],
               aps["identity"], aps["select"], out)
    r = run_bass_kernel_spmd(nc, [{f"in_{name}": a for name, a in arrays.items()}], core_ids=[0])
    return r.results[0]["out"]
```
